# Optimizing a Trainium2 kernel written in Bass

```python
import numpy as np
import jax
import jax.numpy as jnp

def _softmax(x, axis=-1):
    return jax.nn.softmax(x, axis=axis)

def _gelu(x):
    return jax.nn.gelu(x, approximate=True)

def _silu(x):
    return jax.nn.silu(x)

def _sigmoid(x):
    return jax.nn.sigmoid(x)

def _layernorm(x, axis=-1, eps=1e-05):
    m = jnp.mean(x, axis=axis, keepdims=True)
    v = jnp.var(x, axis=axis, keepdims=True)
    return (x - m) / jnp.sqrt(v + eps)

def _scatter_add(tgt, idx, src, axis=0):
    return tgt.at[idx].add(src)

def _segment_sum(src, seg, n):
    return jax.ops.segment_sum(src, seg, n)
kernel_name = 'mk_early_fusion_d1_tok_img256_r4_9a7772'

def setup_inputs(seed: int=0):
    np.random.seed(seed)
    _w = jnp.asarray

    def _rec_inputs():
        import jax
        import jax.numpy as jnp
        _rk = jax.random.key(seed)
        x = 7.22013e-05 + 1.00017 * jax.random.normal(jax.random.fold_in(_rk, 1), (8, 1, 1024, 64), jnp.float32)
        txt = 10 + 10 * jax.random.normal(jax.random.fold_in(_rk, 2), (8, 77, 64), jnp.float32)
        return (x, txt)
    x, txt = _rec_inputs()

    def _L0_tok_setup():
        import jax, jax.numpy as jnp
        import numpy as np
        T, D_IN, D_INT, D_OUT, B = (1024, 64, 64, 64, 8)
        key = jax.random.key(seed)
        ks = jax.random.split(key, 12)
        s_in = 1.0 / np.sqrt(D_IN)
        s_int = 1.0 / np.sqrt(D_INT)
        return {'x_batched': jax.random.normal(ks[0], (B, 1, T, D_IN), dtype=jnp.float32), 'd_gamma_batched': jax.random.uniform(ks[1], (T, T), dtype=jnp.float32), 'Wq': jax.random.uniform(ks[2], (D_IN, D_INT), jnp.float32, -s_in, s_in), 'bq': jax.random.uniform(ks[3], (D_INT,), jnp.float32, -s_in, s_in), 'Wk': jax.random.uniform(ks[4], (D_IN, D_INT), jnp.float32, -s_in, s_in), 'bk': jax.random.uniform(ks[5], (D_INT,), jnp.float32, -s_in, s_in), 'Wv': jax.random.uniform(ks[6], (D_IN, D_INT), jnp.float32, -s_in, s_in), 'bv': jax.random.uniform(ks[7], (D_INT,), jnp.float32, -s_in, s_in), 'Wo': jax.random.uniform(ks[8], (D_INT, D_OUT), jnp.float32, -s_int, s_int), 'bo': jax.random.uniform(ks[9], (D_OUT,), jnp.float32, -s_int, s_int), 'prelu_a': jnp.float32(0.25)}
    _L0_tok_all = _L0_tok_setup()
    _L0_tok_in = {k: v for k, v in _L0_tok_all.items() if k in ('d_gamma_batched', 'Wq', 'bq', 'Wk', 'bk', 'Wv', 'bv', 'Wo', 'bo', 'prelu_a')}
    del _L0_tok_all

    def _L0_attn_setup():
        import jax, jax.numpy as jnp
        import numpy as np
        key = jax.random.key(seed)
        k1, k2, k3 = jax.random.split(key, 3)
        d = 64
        x = jax.random.normal(k1, (8, 512, d), dtype=jnp.float32)
        Wq = jax.random.normal(k2, (d, d), dtype=jnp.float32) * d ** (-0.5)
        Wk = jax.random.normal(k3, (d, d), dtype=jnp.float32) * d ** (-0.5)
        return {'x': x, 'Wq': Wq, 'Wk': Wk}
    _L0_attn_all = _L0_attn_setup()
    _L0_attn_in = {k: v for k, v in _L0_attn_all.items() if k in ('Wq', 'Wk')}
    del _L0_attn_all

    def _L0_ffn_setup():
        import jax, jax.numpy as jnp
        import numpy as np
        B, T, C = (64, 96, 64)
        NH, NKV = (4, 2)
        HD = C // NH
        NREP = NH // NKV
        NE, TOPK = (8, 2)
        HID = int(8 / 3 * C)
        EPS_RMS = 1e-06

        def _rope_tables(t_len):
            inv_freq = 1.0 / 10000.0 ** (np.arange(0, HD, 2, dtype=np.float32) / HD)
            t = np.arange(t_len, dtype=np.float32)
            freqs = np.outer(t, inv_freq)
            emb = np.concatenate([freqs, freqs], axis=-1)
            return (jnp.asarray(np.cos(emb)), jnp.asarray(np.sin(emb)))

        def _rotate_half(x):
            h = x.shape[-1] // 2
            return jnp.concatenate([-x[..., h:], x[..., :h]], axis=-1)

        def _rmsnorm(v, w):
            return v * jax.lax.rsqrt(jnp.mean(v * v, axis=-1, keepdims=True) + EPS_RMS) * w
        key = jax.random.key(seed)
        ks = jax.random.split(key, 10)
        s = lambda k, shape: jax.random.normal(k, shape, jnp.float32) * 0.02
        return {'x': jax.random.normal(ks[0], (B, T, C), jnp.float32), 'ln1_w': jnp.ones((C,), jnp.float32), 'ln2_w': jnp.ones((C,), jnp.float32), 'wq': s(ks[1], (NH * HD, C)), 'wk': s(ks[2], (NKV * HD, C)), 'wv': s(ks[3], (NKV * HD, C)), 'wo': s(ks[4], (C, C)), 'router_w': s(ks[5], (NE, C)), 'w1': s(ks[6], (NE, HID, C)), 'w2': s(ks[7], (NE, C, HID)), 'w3': s(ks[8], (NE, HID, C))}
    _L0_ffn_all = _L0_ffn_setup()
    _L0_ffn_in = {k: v for k, v in _L0_ffn_all.items() if k in ('ln1_w', 'ln2_w', 'wq', 'wk', 'wv', 'wo', 'router_w', 'w1', 'w2', 'w3')}
    del _L0_ffn_all
    return {'x': x, 'txt': txt, 'L0_tok_d_gamma_batched': _L0_tok_in['d_gamma_batched'], 'L0_tok_Wq': _L0_tok_in['Wq'], 'L0_tok_bq': _L0_tok_in['bq'], 'L0_tok_Wk': _L0_tok_in['Wk'], 'L0_tok_bk': _L0_tok_in['bk'], 'L0_tok_Wv': _L0_tok_in['Wv'], 'L0_tok_bv': _L0_tok_in['bv'], 'L0_tok_Wo': _L0_tok_in['Wo'], 'L0_tok_bo': _L0_tok_in['bo'], 'L0_tok_prelu_a': _L0_tok_in['prelu_a'], 'L0_attn_Wq': _L0_attn_in['Wq'], 'L0_attn_Wk': _L0_attn_in['Wk'], 'L0_ffn_ln1_w': _L0_ffn_in['ln1_w'], 'L0_ffn_ln2_w': _L0_ffn_in['ln2_w'], 'L0_ffn_wq': _L0_ffn_in['wq'], 'L0_ffn_wk': _L0_ffn_in['wk'], 'L0_ffn_wv': _L0_ffn_in['wv'], 'L0_ffn_wo': _L0_ffn_in['wo'], 'L0_ffn_router_w': _L0_ffn_in['router_w'], 'L0_ffn_w1': _L0_ffn_in['w1'], 'L0_ffn_w2': _L0_ffn_in['w2'], 'L0_ffn_w3': _L0_ffn_in['w3']}

def reference(x, txt, L0_tok_d_gamma_batched, L0_tok_Wq, L0_tok_bq, L0_tok_Wk, L0_tok_bk, L0_tok_Wv, L0_tok_bv, L0_tok_Wo, L0_tok_bo, L0_tok_prelu_a, L0_attn_Wq, L0_attn_Wk, L0_ffn_ln1_w, L0_ffn_ln2_w, L0_ffn_wq, L0_ffn_wk, L0_ffn_wv, L0_ffn_wo, L0_ffn_router_w, L0_ffn_w1, L0_ffn_w2, L0_ffn_w3):
    import jax
    import jax.numpy as jnp

    def _L0_tok_ref(x_batched, d_gamma_batched, Wq, bq, Wk, bk, Wv, bv, Wo, bo, prelu_a):
        import jax, jax.numpy as jnp
        import numpy as np
        T, D_IN, D_INT, D_OUT, B = (1024, 64, 64, 64, 8)
        x = x_batched.reshape(x_batched.shape[0], T, D_IN)
        q = x @ Wq + bq
        k = x @ Wk + bk
        v = x @ Wv + bv
        scores = jnp.einsum('btd,bsd->bts', q, k)
        retained = jnp.einsum('bts,bsd->btd', d_gamma_batched * scores, v)
        y = retained @ Wo + bo
        out = jnp.where(y >= 0, y, prelu_a * y)
        return out

    def _L0_attn_ref(x, Wq, Wk):
        import jax, jax.numpy as jnp
        import numpy as np
        d = x.shape[-1]
        scale = d ** (-0.5)
        q = jnp.einsum('bnd,ed->bne', x, Wq)
        k = jnp.einsum('bnd,ed->bne', x, Wk)
        sim = jnp.einsum('bid,bjd->bij', q, k) * scale
        attn = jax.nn.softmax(sim, axis=-1)
        out = jnp.einsum('bij,bjd->bid', attn, x)
        return out

    def _L0_ffn_ref(x, ln1_w, ln2_w, wq, wk, wv, wo, router_w, w1, w2, w3):
        import jax, jax.numpy as jnp
        import numpy as np
        B, T, C = (64, 96, 64)
        NH, NKV = (4, 2)
        HD = C // NH
        NREP = NH // NKV
        NE, TOPK = (8, 2)
        HID = int(8 / 3 * C)
        EPS_RMS = 1e-06

        def _rope_tables(t_len):
            inv_freq = 1.0 / 10000.0 ** (np.arange(0, HD, 2, dtype=np.float32) / HD)
            t = np.arange(t_len, dtype=np.float32)
            freqs = np.outer(t, inv_freq)
            emb = np.concatenate([freqs, freqs], axis=-1)
            return (jnp.asarray(np.cos(emb)), jnp.asarray(np.sin(emb)))

        def _rotate_half(x):
            h = x.shape[-1] // 2
            return jnp.concatenate([-x[..., h:], x[..., :h]], axis=-1)

        def _rmsnorm(v, w):
            return v * jax.lax.rsqrt(jnp.mean(v * v, axis=-1, keepdims=True) + EPS_RMS) * w
        Bx, Tx, Cx = x.shape
        h = _rmsnorm(x, ln1_w)
        q = (h @ wq.T).reshape(Bx, Tx, NH, HD).transpose(0, 2, 1, 3)
        k = (h @ wk.T).reshape(Bx, Tx, NKV, HD).transpose(0, 2, 1, 3)
        v = (h @ wv.T).reshape(Bx, Tx, NKV, HD).transpose(0, 2, 1, 3)
        cos, sin = _rope_tables(Tx)
        cos, sin = (cos[None, None], sin[None, None])
        q = q * cos + _rotate_half(q) * sin
        k = k * cos + _rotate_half(k) * sin
        k = jnp.repeat(k, NREP, axis=1)
        v = jnp.repeat(v, NREP, axis=1)
        scores = jnp.einsum('bhtd,bhsd->bhts', q, k) / jnp.sqrt(jnp.float32(HD))
        causal = jnp.tril(jnp.ones((Tx, Tx), dtype=bool))
        scores = jnp.where(causal[None, None], scores, jnp.float32(-1e+30))
        att = jax.nn.softmax(scores, axis=-1)
        y = jnp.einsum('bhts,bhsd->bhtd', att, v).transpose(0, 2, 1, 3).reshape(Bx, Tx, Cx)
        x = x + y @ wo.T
        flat = _rmsnorm(x, ln2_w).reshape(-1, Cx)
        probs = jax.nn.softmax(flat @ router_w.T, axis=-1)
        tp, ti = jax.lax.top_k(probs, TOPK)
        tp = tp / (jnp.sum(tp, axis=-1, keepdims=True) + 1e-09)
        weights = jnp.sum(tp[..., None] * jax.nn.one_hot(ti, NE, dtype=flat.dtype), axis=1)
        out = jnp.zeros_like(flat)
        for e in range(NE):
            hh = jax.nn.silu(flat @ w1[e].T) * (flat @ w3[e].T)
            out = out + weights[:, e:e + 1] * (hh @ w2[e].T)
        return x + out.reshape(Bx, Tx, Cx)
    h = _L0_tok_ref(x, L0_tok_d_gamma_batched, L0_tok_Wq, L0_tok_bq, L0_tok_Wk, L0_tok_bk, L0_tok_Wv, L0_tok_bv, L0_tok_Wo, L0_tok_bo, L0_tok_prelu_a)
    h = jnp.concatenate([h, txt], axis=1)
    h = h + _L0_attn_ref(_layernorm(h, axis=-1), L0_attn_Wq, L0_attn_Wk)
    h = h + _L0_ffn_ref(_layernorm(h, axis=-1), L0_ffn_ln1_w, L0_ffn_ln2_w, L0_ffn_wq, L0_ffn_wk, L0_ffn_wv, L0_ffn_wo, L0_ffn_router_w, L0_ffn_w1, L0_ffn_w2, L0_ffn_w3)
    return h

_drawn_inputs = setup_inputs


def setup_inputs(seed=0):
    import zlib

    import numpy as np

    out = dict(_drawn_inputs(seed))
    spreads = {'L0_ffn_ln1_w': (1.0, 0.6), 'L0_ffn_ln2_w': (1.0, 0.6)}
    factors = {'L0_tok_bo': 32.685,
     'L0_attn_Wq': 8.0,
     'L0_attn_Wk': 8.0,
     'L0_ffn_wq': 8.0,
     'L0_ffn_wk': 8.0,
     'L0_ffn_wv': 8.0,
     'L0_ffn_wo': 8.0,
     'L0_ffn_router_w': 8.0,
     'L0_ffn_w1': 8.0,
     'L0_ffn_w2': 8.0,
     'L0_ffn_w3': 8.0}
    for name, (base, spread) in spreads.items():
        noise = np.random.default_rng([zlib.crc32(name.encode()), seed]).standard_normal(out[name].shape)
        drawn = base * np.exp(spread * noise) if base else spread * noise
        out[name] = jnp.asarray(drawn.astype(out[name].dtype))
    for name, factor in factors.items():
        out[name] = (out[name] * factor).astype(out[name].dtype)
    return out
```

```python
import concourse.bass as bass
from concourse import mybir
from contextlib import ExitStack

F32 = mybir.dt.float32
FR = mybir.dt.float32r
BF = mybir.dt.bfloat16
ALU = mybir.AluOpType
ACT = mybir.ActivationFunctionType
AX = mybir.AxisListType

P = 128
B, T_IMG, C = 8, 1024, 64
T_TXT = 77
T = T_IMG + T_TXT
NT = 9
TP = NT * P
NTI = T_IMG // P
LAST = T - NTI * P
HALF = 512
NC3 = 3
CW = 3 * P
JW = T // 3
NH, NKV, HD = 4, 2, 16
NE, HID = 8, 170
FH = NE * HID
NG = (FH + P - 1) // P
GW = [min(P, FH - P * g) for g in range(NG)]
KEYS = [P] * NTI + [LAST]
LN_EPS, RMS_EPS = 1e-5, 1e-6
CHUNKS = [(1, 256), (1, 256), (1, 384), (1, 512), (2, 320), (2, 384), (2, 448), (2, 512), (3, 368)]


def early_fusion_kernel(nc, x, txt, gamma, tWq, tbq, tWk, tbk, tWv, tbv, tWo, tbo, prelu_a, aWq, aWk,
                        ln1_w, ln2_w, wq, wk, wv, wo, router_w, w1, w2, w3,
                        c_ident, c_mask, c_cos, c_sin, c_sel, c_tri, out):
    ctx = ExitStack()
    with ctx:
        def sb(name, shape, dt=F32):
            return ctx.enter_context(nc.sbuf_tensor(name, shape, dt))

        sem_nums = []

        def sem(name):
            s = ctx.enter_context(nc.semaphore(name))
            sem_nums.append(s.num)
            return s

        def f(ap):
            return ap.bitcast(F32)

        def r(ap):
            return ap.bitcast(FR)

        def spread(ap, n):
            return ap.unsqueeze(2).broadcast_to([ap.shape[0], ap.shape[1], n])

        def every(ap, n):
            return ap.unsqueeze(1).broadcast_to([ap.shape[0], n, ap.shape[1]])

        ident = sb("ident", [P, P])
        identb = sb("identb", [P, P], BF)
        maskb = sb("maskb", [P, 2, P], BF)
        cos = sb("cos", [P, NT, HD])
        sin = sb("sin", [P, NT, HD])
        tri = sb("tri", [P, NE * NE])
        sel = sb("sel", [16, NG * P], FR)
        gT = sb("gT", [P, NTI, T_IMG])
        bq_c = sb("bq_c", [P, 1])
        bk_c = sb("bk_c", [P, 1])
        bv_c = sb("bv_c", [C, 1])
        bo_c = sb("bo_c", [C, 1])
        nbo_c = sb("nbo_c", [C, 1])
        na_c = sb("na_c", [C, 1])
        nhalf = sb("nhalf", [P, 1])
        bv_row = sb("bv_row", [P, C])
        ln1_b = sb("ln1_b", [P, C])
        ln2_b = sb("ln2_b", [P, C])
        tq_s = sb("tq_s", [P, 2, P], FR)
        tk_s = sb("tk_s", [P, 2, P], FR)
        vo_s = sb("vo_s", [P, 2, 256], FR)
        a_s = sb("a_s", [P, 2, P], FR)
        qkv_f = sb("qkv_f", [P, 256])
        qkv_s = sb("qkv_s", [P, 2, 256], FR)
        wo_s = sb("wo_s", [P, 2, 256], FR)
        rw_s = sb("rw_s", [P, 2, 256], FR)
        w1_s = sb("w1_s", [P, 2, NG * P], FR)
        w3_s = sb("w3_s", [P, 2, NG * P], FR)
        w2_s = sb("w2_s", [P, NG, C])

        class Region:
            def __init__(self, tensor, at):
                self.tensor, self.at = tensor, at

            def take(self, parts, *shape):
                n = 1
                for d in shape:
                    n *= d
                ap = self.tensor[0:parts, self.at:self.at + n]
                self.at += n
                if len(shape) == 2:
                    return ap.rearrange("p (a b) -> p a b", b=shape[1])
                if len(shape) == 3:
                    return ap.rearrange("p (a b c) -> p a b c", b=shape[1], c=shape[2])
                return ap

        region = sb("region", [P, 7248])
        prep = Region(region, 0)
        maskf = prep.take(P, 2, P)
        sel_f = prep.take(16, NG * P)
        g_row = prep.take(P, 2, T_IMG)
        stage = prep.take(P, 6, P)
        wstage = prep.take(P, NG, 2, C)
        w2stage = prep.take(C, FH)
        mixing = Region(region, 0)
        neg = mixing.take(C, T_IMG)
        yT = mixing.take(C, T_IMG)
        rest = Region(region, 0)
        rot = rest.take(P, 2, NT, 96)
        qk = rest.take(P, NT, 96)
        qkh = rest.take(P, NT, 96)
        qkl = rest.take(P, NT, 96)
        cmp = rest.take(P, 2, NT, NE * NE)
        R1 = rest.take(P, NT, C)
        hn = rest.take(P, NT, C)
        Y = rest.take(P, NT, C)

        xin = sb("xin", [P, NTI, C])
        hi_lo = sb("hi_lo", [P, NT, 2, C])
        fT = sb("fT", [P, TP], FR)
        ka = sb("ka", [P, TP], FR)
        xb = sb("xb", [P, TP], FR)
        vt = sb("vt", [P, NTI, C])
        ring = sb("ring", [P, 4, HALF])
        hid = sb("hid", [P, 2, CW])
        H = sb("H", [P, NT, C])
        H2 = sb("H2", [P, NT, C])
        xc = sb("xc", [P, NT, C])
        sq = sb("sq", [P, NT, C])
        st = sb("st", [P, 8, NT])
        xv = sb("xv", [P, NT, 66])
        nm = sb("nm", [P, NT])
        oT = sb("oT", [P, TP])
        rden = sb("rden", [P, NT, NH])
        qp = sb("qp", [P, NT, NH, 4, 32])
        kp = sb("kp", [P, NT, 4, 32])
        qT = sb("qT", [P, NH, TP], FR)
        qa, qb = qT[:, 0, :], qT[:, 1, :]
        mp = qp[:, :, 0, 0:3, :].rearrange("p t a b -> p t (a b)")
        vv = sb("vv", [P, NT, NKV, 32])
        nm4 = sb("nm4", [P, NH, NT])
        lg = sb("lg", [P, NT, NE])
        pr = sb("pr", [P, NT, NE])
        wt = sb("wt", [P, NT, NE])
        wp = sb("wp", [P, NT, 16])
        wT = sb("wT", [16, TP], FR)

        PS = ctx.enter_context(nc.psum_tensor("PS", [P, 8, HALF], F32))

        p_in = sem("p_in")
        p_g = [sem("p_g0"), sem("p_g1")]
        p_set = sem("p_set")
        p_pe = sem("p_pe")
        p_dv = sem("p_dv")
        p_gt = sem("p_gt")
        p_gc = sem("p_gc")
        NIN = [0]

        with nc.Block() as block:
            @block.sync
            def _(sp):
                def load(dst, src):
                    sp.dma_start(dst, src).then_inc(p_in, 16)
                    NIN[0] += 1

                load(ident[:, :], c_ident)
                load(maskf, c_mask)
                load(cos[:, :, :], c_cos)
                load(sin[:, :, :], c_sin)
                load(sel_f[:, :], c_sel)
                load(tri[:, :], c_tri)
                col = lambda v: v.rearrange("(n a) -> n a", a=1)
                row = lambda v: v.rearrange("(a n) -> a n", a=1)
                for h in range(2):
                    hs = slice(C * h, C * h + C)
                    load(bq_c[hs, :], col(tbq))
                    load(bk_c[hs, :], col(tbk))
                    load(stage[hs, 0, 0:C], tWq)
                    load(stage[hs, 1, 0:C], tWk)
                    load(stage[0:64, 3, hs], wq)
                    load(stage[64:96, 3, hs], wk)
                    load(stage[96:128, 3, hs], wv)
                    load(stage[0:C, 4, hs], wo)
                    load(stage[0:NE, 5, hs], router_w)
                load(bv_c[:, :], col(tbv))
                load(bo_c[:, :], col(tbo))
                load(na_c[:, :], prelu_a.broadcast_to([C, 1]))
                load(ln1_b[:, :], row(ln1_w).broadcast_to([P, C]))
                load(ln2_b[:, :], row(ln2_w).broadcast_to([P, C]))
                load(stage[0:C, 2, 0:C], tWv)
                load(stage[0:C, 2, C:P], tWo)
                load(ring[0:C, 0, 0:C], aWq)
                load(ring[0:C, 0, C:P], aWk)
                load(w2stage[:, :].rearrange("c (e k) -> c e k", e=NE), w2.rearrange("e c k -> c e k"))
                for n, w in enumerate((w1, w3)):
                    rows = w.rearrange("e k c -> (e k) c")
                    if n == 1:
                        sp.wait_ge(p_dv, 1)
                    for h in range(2):
                        load(wstage[:, 0:NG - 1, h, :], rows[0:(NG - 1) * P, :].rearrange("(g p) c -> p g c", p=P))
                        load(wstage[0:GW[-1], NG - 1, h, :], rows[(NG - 1) * P:FH, :])
                for t in range(NTI):
                    if t >= 2:
                        sp.wait_ge(p_gc, 2 * (t - 1))
                    sp.dma_start(g_row[:, t % 2, :], gamma[t * P:(t + 1) * P, :]).then_inc(p_g[t % 2], 16)


            @block.gpsimd
            def _(pool):
                for m in (H, H2, hi_lo, xv, qp, kp, vv, wp):
                    flat = m[:]
                    pool.memset(flat, 0.0).then_inc(p_set, 1)
                pool.memset(f(vo_s[:, :, :]), 0.0).then_inc(p_set, 1)
                pool.memset(f(wo_s[:, :, :]), 0.0).then_inc(p_set, 1)
                pool.memset(f(rw_s[:, :, :]), 0.0).then_inc(p_set, 1)
                pool.memset(f(xb[:, :]), 0.0).then_inc(p_set, 1)
                pool.memset(qkv_f[:, :], 0.0).then_inc(p_set, 1)
                pool.memset(nhalf[:, :], -0.5).then_inc(p_set, 1)
                pool.wait_ge(p_set, 14)
                pool.memset(f(xb[64:66, :]), 1.0).then_inc(p_set, 1)
                pool.wait_ge(p_set, 15)
                pool.memset(xv[:, :, 64:65], 1.0).then_inc(p_set, 1)
                pool.memset(kp[:, :, 3, 0:2], 1.0).then_inc(p_set, 1)
                pool.memset(vv[:, :, :, 16:17], 1.0).then_inc(p_set, 1)

            @block.tensor
            def _(pe):
                pe.wait_ge(p_in, 16 * (NIN[0] - 4))
                def rows_T(n):
                    for g in range(NG):
                        m = pe.transpose(PS[:, 4 * n + g // 4, (g % 4) * P:(g % 4) * P + GW[g]],
                                         wstage[0:GW[g], g, :, :].rearrange("p a c -> p (a c)"),
                                         ident[0:GW[g], 0:GW[g]])
                    m.then_inc(p_pe, 1)

                rows_T(0)
                pe.wait_ge(p_in, 16 * NIN[0])
                rows_T(1)
                pe.wait_ge(p_dv, 2)
                pe.transpose(PS[:, 0, 0:P], stage[:, 3, :], ident[:, :])
                pe.transpose(PS[:, 0, P:P + C], stage[0:C, 4, :], ident[0:C, 0:C])
                pe.transpose(PS[:, 0, 256:256 + NE], stage[0:NE, 5, :], ident[0:NE, 0:NE])
                pe.transpose(PS[0:C, 0, 384:384 + C], stage[0:C, 2, 0:C], ident[0:C, 0:C]).then_inc(p_pe, 1)
                pe.wait_ge(p_dv, 3)
                pe.matmul(PS[:, 1, 0:C], ring[0:C, 1, 0:P], stage[0:C, 2, C:P], start=True, stop=True)
                pe.matmul(PS[:, 1, C:P], ring[0:C, 1, P:2 * P], ring[0:C, 0, C:P], start=True, stop=True)
                pe.matmul(PS[:, 1, P:P + C], ring[0:C, 1, 256:384], stage[0:C, 2, C:P],
                          start=True, stop=True).then_inc(p_pe, 1)
                for g in range(NG):
                    m = pe.transpose(PS[0:GW[g], 2 + g // 8, (g % 8) * C:(g % 8) * C + C],
                                     w2stage[:, g * P:g * P + GW[g]], ident[0:C, 0:C])
                m.then_inc(p_pe, 1)
                for t in range(NTI):
                    pe.wait_ge(p_g[t % 2], 16 * (t // 2 + 1))
                    for h in range(2):
                        n = 2 * t + h
                        if n >= 2:
                            pe.wait_ge(p_gc, n - 1)
                        if n == 0:
                            pe.wait_ge(p_dv, 2)
                        for s in range(4):
                            m = pe.transpose(PS[:, 4 + n % 2, s * P:(s + 1) * P],
                                             g_row[:, t % 2, (4 * h + s) * P:(4 * h + s + 1) * P], ident[:, :])
                        m.then_inc(p_gt, 1)

            @block.vector
            def _(dve):
                chain = [0]
                p_ch = sem("p_ch")

                def link(ins):
                    chain[0] += 1
                    ins.then_inc(p_ch, 1)
                    dve.wait_ge(p_ch, chain[0])

                def split(dst, src):
                    h, low = dst
                    link(dve.tensor_copy(h, src))
                    return dve.tensor_tensor(low, src, f(h), ALU.subtract)

                dve.wait_ge(p_set, 18)
                dve.wait_ge(p_in, 16 * (NIN[0] - 4))
                for n, w in enumerate((w1_s, w3_s)):
                    dve.wait_ge(p_pe, n + 1)
                    for g in range(NG):
                        src = PS[:, 4 * n + g // 4, (g % 4) * P:(g % 4) * P + GW[g]]
                        last = split((w[:, 0, g * P:g * P + GW[g]], w[:, 1, g * P:g * P + GW[g]]), src)
                    last.then_inc(p_dv, 1)
                dve.tensor_copy(identb[:, :], ident[:, :])
                dve.tensor_copy(maskb[:, :, :], maskf[:, :, :])
                dve.tensor_copy(sel[:, :], sel_f[:, :])
                link(dve.tensor_scalar(nbo_c[:, :], bo_c[:, :], -1.0, None, ALU.mult))
                link(dve.tensor_scalar(na_c[:, :], na_c[:, :], -1.0, None, ALU.mult))
                for w, k in ((tq_s, 0), (tk_s, 1)):
                    for h in range(2):
                        hs = slice(C * h, C * h + C)
                        split((w[:, 0, hs], w[:, 1, hs]), stage[:, k, 0:C])
                dve.wait_ge(p_pe, 3)
                dve.tensor_copy(qkv_f[:, 0:P], PS[:, 0, 0:P])
                src = PS[:, 0, 0:96].rearrange("p (h a b) -> p h a b", h=6, a=2)
                dst = qkv_f[:, P:P + 96].rearrange("p (h a b) -> p h a b", h=6, a=2)
                dve.tensor_scalar(dst[:, :, 0, :], src[:, :, 1, :], -1.0, None, ALU.mult)
                link(dve.tensor_copy(dst[:, :, 1, :], src[:, :, 0, :]))
                split((qkv_s[:, 0, :], qkv_s[:, 1, :]), qkv_f[:, :])
                split((wo_s[:, 0, 0:C], wo_s[:, 1, 0:C]), PS[:, 0, P:P + C])
                split((rw_s[:, 0, 0:NE], rw_s[:, 1, 0:NE]), PS[:, 0, 256:256 + NE])
                for h in range(2):
                    hs = slice(C * h, C * h + C)
                    dve.tensor_copy(ring[0:C, 1, hs], PS[0:C, 0, 384:384 + C])
                    dve.tensor_copy(ring[0:C, 1, P + C * h:P + C * h + C], ring[0:C, 0, 0:C])
                dve.tensor_copy(ring[0:C, 1, 256:384], bv_c[:, 0:1].broadcast_to([C, P])).then_inc(p_dv, 1)
                dve.wait_ge(p_pe, 4)
                split((vo_s[:, 0, 0:C], vo_s[:, 1, 0:C]), PS[:, 1, 0:C])
                for h in range(2):
                    hs = slice(C * h, C * h + C)
                    split((a_s[:, 0, hs], a_s[:, 1, hs]), PS[:, 1, C:P])
                dve.tensor_copy(bv_row[:, :], PS[:, 1, P:P + C])
                dve.wait_ge(p_pe, 5)
                dve.tensor_copy(w2_s[:, 0:8, :], PS[:, 2, :].rearrange("p (g c) -> p g c", g=8))
                dve.tensor_copy(w2_s[:, 8:10, :], PS[:, 3, 0:2 * C].rearrange("p (g c) -> p g c", g=2))
                dve.tensor_copy(w2_s[0:GW[-1], 10, :], PS[0:GW[-1], 3, 2 * C:3 * C])

            @block.scalar
            def _(act):
                for n in range(2 * NTI):
                    t, h = n // 2, n % 2
                    act.wait_ge(p_gt, n + 1)
                    act.activation(gT[:, 4 * h:4 * h + 4, t * P:(t + 1) * P],
                                   PS[:, 4 + n % 2, :].rearrange("p (s c) -> p s c", s=4), ACT.Copy).then_inc(p_gc, 1)

        first_loop_sem = len(sem_nums)
        x_in = sem("x_in")
        stored = sem("stored")
        x_split = sem("x_split")
        x_turned = sem("x_turned")
        x_cols = sem("x_cols")
        q_sum = sem("q_sum")
        q_hi = sem("q_hi")
        q_lo = sem("q_lo")
        k_sum = sem("k_sum")
        k_hi = sem("k_hi")
        k_lo = sem("k_lo")
        v_sum = sem("v_sum")
        v_out = sem("v_out")
        ts_sum = sem("ts_sum")
        gated = sem("gated")
        mixed = sem("mixed")
        y_parts = sem("y_parts")
        y_cols = sem("y_cols")
        y_turned = sem("y_turned")
        h_rows = sem("h_rows")
        norm_sum = sem("norm_sum")
        norm_root = sem("norm_root")
        pool_step = sem("pool_step")
        a_split = sem("a_split")
        a_turned = sem("a_turned")
        a_cols = sem("a_cols")
        a_copy = sem("a_copy")
        aq_sum = sem("aq_sum")
        aq_hi = sem("aq_hi")
        aq_lo = sem("aq_lo")
        as_sum = sem("as_sum")
        as_max = sem("as_max")
        am_split = sem("am_split")
        am_turned = sem("am_turned")
        am_rows = sem("am_rows")
        at_sum = sem("at_sum")
        at_exp = sem("at_exp")
        av_part = sem("av_part")
        av_sum = sem("av_sum")
        av_copy = sem("av_copy")
        av_turned = sem("av_turned")
        av_rows = sem("av_rows")
        b_split = sem("b_split")
        b_turned = sem("b_turned")
        b_cols = sem("b_cols")
        b_proj = sem("b_proj")
        b_rope = sem("b_rope")
        b_v = sem("b_v")
        b_qk = sem("b_qk")
        b_slot_dve = sem("b_slot_dve")
        b_slot_pool = sem("b_slot_pool")
        bt_turned = sem("bt_turned")
        bt_cols = sem("bt_cols")
        bs_sum = sem("bs_sum")
        bs_max = sem("bs_max")
        bm_split = sem("bm_split")
        bm_turned = sem("bm_turned")
        bm_rows = sem("bm_rows")
        bx_sum = sem("bx_sum")
        bx_exp = sem("bx_exp")
        bv_part = sem("bv_part")
        bv_sum = sem("bv_sum")
        bv_copy = sem("bv_copy")
        bv_turned = sem("bv_turned")
        bv_rows = sem("bv_rows")
        o_split = sem("o_split")
        o_turned = sem("o_turned")
        o_cols = sem("o_cols")
        o_proj = sem("o_proj")
        o_rows = sem("o_rows")
        f_split = sem("f_split")
        f_turned = sem("f_turned")
        f_cols = sem("f_cols")
        r_proj = sem("r_proj")
        r_in = sem("r_in")
        r_exp = sem("r_exp")
        w_split = sem("w_split")
        w_turned = sem("w_turned")
        w_cols = sem("w_cols")
        e_sum = sem("e_sum")
        e_silu = sem("e_silu")
        e_mul = sem("e_mul")
        e_hid = sem("e_hid")
        e_part = sem("e_part")
        e_out = sem("e_out")
        e_copy = sem("e_copy")
        e_turned = sem("e_turned")
        e_rows = sem("e_rows")
        hr_done = sem("hr_done")
        dve_step = sem("dve_step")
        loop_sems = sem_nums[first_loop_sem:]
        assert loop_sems == list(range(loop_sems[0], loop_sems[0] + len(loop_sems))) or \
            loop_sems == list(range(loop_sems[0], loop_sems[0] - len(loop_sems), -1))

        def tile(t):
            return slice(t * P, (t + 1) * P)

        def cols(c):
            return slice(c * CW, (c + 1) * CW)

        def kept(c, jt):
            off = max(0, (jt - 3 * c) * P)
            return off, min(off, CW - 256)

        with nc.Fori(0, B) as b:
            with nc.Block() as block:
                @block.sync
                def _(sp):
                    sp.dma_start(xin[:, :, :], x[bass.ds(b, 1), :, :, :].rearrange("a o (t p) f -> p (a o t) f", p=P))\
                        .then_inc(x_in, 16)
                    sp.dma_start(H[0:LAST, NTI, :], txt[bass.ds(b, 1), :, :].rearrange("a t f -> (a t) f"))\
                        .then_inc(x_in, 16)
                    sp.wait_ge(e_rows, NC3)
                    sp.dma_start(out[bass.ds(b, 1), 0:T_IMG, :].rearrange("a (t p) f -> p (a t) f", p=P),
                                 sq[:, 0:NTI, :]).then_inc(stored, 16)
                    sp.dma_start(out[bass.ds(b, 1), T_IMG:T, :].rearrange("a t f -> (a t) f"),
                                 sq[0:LAST, NTI, :]).then_inc(stored, 16)
                    sp.wait_ge(stored, 32)

                @block.gpsimd
                def _(pool):
                    steps = [0]

                    def root(n, eps):
                        pool.wait_ge(norm_sum, n + 1)
                        pool.tensor_scalar(st[:, 2, :], st[:, 1, :], 1.0 / C, eps, ALU.mult, ALU.add).then_inc(pool_step, 1)
                        steps[0] += 1
                        pool.wait_ge(pool_step, steps[0])
                        pool.tensor_tensor(st[:, 3, :], st[:, 2, :], nhalf[:, 0:1].broadcast_to([P, NT]), ALU.pow)\
                            .then_inc(norm_root, 1)

                    root(0, LN_EPS)
                    root(1, LN_EPS)
                    root(2, RMS_EPS)
                    pool.wait_ge(b_qk, 2)
                    pool.tensor_copy(kp[:, :, 0, :], qkh[:, :, 64:96]).then_inc(b_slot_pool, 1)
                    pool.tensor_copy(kp[:, :, 1, :], qkl[:, :, 64:96]).then_inc(b_slot_pool, 1)
                    pool.tensor_copy(kp[:, :, 2, :], qkh[:, :, 64:96]).then_inc(b_slot_pool, 1)
                    for n in range(NH):
                        o = HD * (n // 2)
                        pool.tensor_copy(qp[:, :, n, 2, o:o + HD], qkl[:, :, n * HD:(n + 1) * HD]).then_inc(b_slot_pool, 1)
                    root(3, RMS_EPS)
                    pool.wait_ge(o_rows, 5)
                    pool.tensor_tensor(H[:, :, :], H2[:, :, :], R1[:, :, :], ALU.add).then_inc(hr_done, 1)

                @block.tensor
                def _(pe):
                    def turn3(src, counted, free=None):
                        for t in range(NT):
                            m = pe.transpose(PS[:, t // 3, tile(t % 3)], src(t), ident[:, :])
                            if t % 3 == 2:
                                m.then_inc(counted, 1)

                    def both(o, lhs, rhs, **k):
                        pe.matmul(o, lhs[0], rhs[0], start=True, stop=False)
                        return pe.matmul(o, lhs[1], rhs[1], start=False, stop=True)

                    pe.wait_ge(x_split, 2)
                    for t in range(NTI):
                        m = pe.transpose(PS[:, t // 4, tile(t % 4)], hi_lo[:, t, :, :].rearrange("p a c -> p (a c)"), ident[:, :])
                        if t % 4 == 3:
                            m.then_inc(x_turned, 1)
                    for c in range(2):
                        pe.wait_ge(x_cols, c + 1)
                        cs = slice(c * HALF, (c + 1) * HALF)
                        both(PS[:, 4 + c, :], (tk_s[:, 0, :], tk_s[:, 1, :]), (fT[:, cs],) * 2).then_inc(k_sum, 1)
                        both(PS[:, 2 + c, :], (tq_s[:, 0, :], tq_s[:, 1, :]), (fT[:, cs],) * 2).then_inc(q_sum, 1)
                    for s in range(NTI):
                        bank = (6, 7, 0, 1)[s // 2]
                        m = both(PS[:, bank, 256 * (s % 2):256 * (s % 2) + 256], (fT[:, tile(s)],) * 2,
                                 (vo_s[:, 0, :], vo_s[:, 1, :]))
                        if s % 2:
                            m.then_inc(v_sum, 1)

                    def scores(n):
                        c, s = n // NTI, n % NTI
                        if n < 4:
                            pe.wait_ge(q_lo, min(2, n + 1))
                            pe.wait_ge(k_lo, 2 if n >= 2 else 1)
                        if n == 0:
                            pe.wait_ge(k_lo, 2)
                            pe.wait_ge(q_lo, 2)
                        if n >= 4:
                            pe.wait_ge(gated, n - 3)
                        cs = slice(c * HALF, (c + 1) * HALF)
                        both(PS[:, 2 + n % 4, :], (ka[:, tile(s)],) * 2, (qa[:, cs], qb[:, cs])).then_inc(ts_sum, 1)

                    def mix(n):
                        c, s = n // NTI, n % NTI
                        if n == 0:
                            pe.wait_ge(v_out, 4)
                        pe.wait_ge(gated, n + 1)
                        pe.matmul(PS[0:C, 6 + c, :], vt[:, s, :], ring[:, n % 4, :], start=(s == 0), stop=(s == NTI - 1))\
                            .then_inc(mixed, 1)

                    for n in range(2 * NTI + 2):
                        if n < 2 * NTI:
                            scores(n)
                        if n >= 2:
                            mix(n - 2)
                    for t in range(NTI):
                        if t % 4 == 0:
                            pe.wait_ge(y_cols, t // 4 + 1)
                        m = pe.transpose(PS[:, 0, C * t:C * t + C], yT[:, tile(t)], ident[0:C, 0:C])
                    m.then_inc(y_turned, 1)

                    pe.wait_ge(a_split, 2)
                    turn3(lambda t: hi_lo[:, t, :, :].rearrange("p a c -> p (a c)"), a_turned)
                    for c in range(NC3):
                        pe.wait_ge(a_cols, c + 1)
                        both(PS[:, 3 + c, 0:CW], (a_s[:, 0, :], a_s[:, 1, :]), (ka[:, cols(c)],) * 2).then_inc(aq_sum, 1)
                    pe.wait_ge(aq_hi, NC3)
                    pe.wait_ge(aq_lo, NC3)
                    pe.wait_ge(a_copy, 1)
                    for t in range(NT):
                        if t >= 2:
                            pe.wait_ge(as_max, t - 1)
                        for j in range(3):
                            js = slice(JW * j, JW * j + JW + 1)
                            m = both(PS[:, 3 * (t % 2) + j, 0:JW + 1], (qa[:, tile(t)], qb[0:C, tile(t)]),
                                     (ka[:, js], xb[0:C, js]))
                        m.then_inc(as_sum, 1)
                    for c in range(NC3):
                        pe.wait_ge(am_split, c + 1)
                        if c >= 1:
                            pe.wait_ge(am_rows, c)
                        for t in range(3):
                            m = pe.transpose(PS[0:96, 6, tile(t)], mp[:, 3 * c + t, :], ident[:, :])
                        m.then_inc(am_turned, 1)

                    def at_scores(n):
                        c, jt = n // NT, n % NT
                        if jt == 0:
                            pe.wait_ge(am_rows, c + 1)
                        if n == 0:
                            pe.wait_ge(as_max, NT)
                        if n >= 4:
                            pe.wait_ge(at_exp, n - 3)
                        both(PS[:, n % 4, 0:CW], (ka[:, tile(jt)], xb[0:66, tile(jt)]),
                             (qa[:, cols(c)], qb[0:66, cols(c)])).then_inc(at_sum, 1)

                    def at_values(n):
                        c, jt = n // NT, n % NT
                        pe.wait_ge(at_exp, n + 1)
                        if jt == 0 and c == 2:
                            pe.wait_ge(av_copy, 1)
                        k = KEYS[jt]
                        m = pe.matmul(PS[0:66, 4 + c % 2, 0:CW], xv[0:k, jt, :], ring[0:k, n % 4, 0:CW],
                                      start=(jt == 0), stop=(jt == NT - 1)).then_inc(av_part, 1)
                        if jt == NT - 1:
                            turn_values.append(c)

                    turn_values = []

                    def at_turn(c):
                        pe.wait_ge(av_copy, c + 1)
                        if c >= 1:
                            pe.wait_ge(av_rows, c)
                        for t in range(3):
                            m = pe.transpose(PS[:, 7, 66 * t:66 * t + 66], oT[0:66, tile(3 * c + t)], ident[0:66, 0:66])
                        m.then_inc(av_turned, 1)

                    for n in range(3 * NT + 2):
                        if n < 3 * NT:
                            at_scores(n)
                        if n >= 2:
                            at_values(n - 2)
                        if n >= 2 and (n - 2) % NT == 3 and n - 2 > NT:
                            at_turn((n - 2) // NT - 1)
                    at_turn(2)

                    pe.wait_ge(b_split, 2)
                    turn3(lambda t: hi_lo[:, t, :, :].rearrange("p a c -> p (a c)"), b_turned)
                    for t in range(NT):
                        pe.wait_ge(b_cols, t // 3 + 1)
                        m = both(PS[:, 3 + t // 2, 256 * (t % 2):256 * (t % 2) + 256], (fT[:, tile(t)],) * 2,
                                 (qkv_s[:, 0, :], qkv_s[:, 1, :]))
                        if t % 2 or t == NT - 1:
                            m.then_inc(b_proj, 1)
                    for n in range(1 + NH):
                        for c in range(3):
                            u = 3 * n + c
                            if u == 0:
                                pe.wait_ge(b_slot_dve, 4)
                                pe.wait_ge(b_slot_pool, 7)
                            if u >= 3:
                                pe.wait_ge(bt_cols, u - 2)
                            for t in range(3 * c, 3 * c + 3):
                                src = kp[:, t, :, :] if n == 0 else qp[:, t, n - 1, :, :]
                                m = pe.transpose(PS[:, u % 3, tile(t % 3)], src.rearrange("p a b -> p (a b)"), ident[:, :])
                            m.then_inc(bt_turned, 1)
                    pe.wait_ge(bt_cols, 15)
                    for n in range(NH):
                        for t in range(NT):
                            u = NT * n + t
                            if u >= 2:
                                pe.wait_ge(bs_max, u - 1)
                            count, wide = CHUNKS[t]
                            diag = P if t < NT - 1 else 3 * 368 - NTI * P
                            for j in range(count):
                                o = PS[:, 3 * (u % 2) + j, 0:wide]
                                last = j == count - 1
                                m = pe.matmul(o, qT[0:96, n, tile(t)], ka[0:96, wide * j:wide * j + wide],
                                              start=True, stop=not last)
                            at = t * P - wide * (count - 1)
                            m = pe.matmul(PS[:, 3 * (u % 2) + count - 1, at:at + diag], identb[:, :], maskb[:, 0, 0:diag],
                                          start=False, stop=True)
                            m.then_inc(bs_sum, 1)
                    for n in range(NH):
                        pe.wait_ge(bm_split, n + 1)
                        for c in range(3):
                            u = 3 * n + c
                            if u >= 2:
                                pe.wait_ge(bm_rows, u - 1)
                            for t in range(3):
                                m = pe.transpose(PS[:, 6 + u % 2, tile(t)],
                                                 qp[:, 3 * c + t, n, :, :].rearrange("p a b -> p (a b)"), ident[:, :])
                            m.then_inc(bm_turned, 1)

                    steps = [(c, n, jt) for c in range(3) for n in range(NH) for jt in range(3 * c + 3)]

                    def b_scores(u):
                        c, n, jt = steps[u]
                        if u == 0:
                            pe.wait_ge(bm_rows, 3 * NH)
                        if u >= 4:
                            pe.wait_ge(bx_exp, u - 3)
                        keep, o = kept(c, jt)
                        masked = jt >= 3 * c
                        m = pe.matmul(PS[:, u % 4, o:CW], ka[0:98, tile(jt)], qT[0:98, n, c * CW + o:(c + 1) * CW],
                                      start=True, stop=not masked)
                        if masked:
                            m = pe.matmul(PS[:, u % 4, keep:keep + P], identb[:, :], maskb[:, 1, :], start=False, stop=True)
                        m.then_inc(bx_sum, 1)

                    def b_values(u):
                        c, n, jt = steps[u]
                        pe.wait_ge(bx_exp, u + 1)
                        if c == 2 and n == 0 and jt == 0:
                            pe.wait_ge(bv_copy, 1)
                        keep, _ = kept(c, jt)
                        k = KEYS[jt]
                        m = pe.matmul(PS[32 * n:32 * n + 32, 6 + c % 2, keep:CW], vv[0:k, jt, n // 2, :],
                                      ring[0:k, u % 4, keep:CW], start=(jt == 0), stop=(jt == 3 * c + 2))
                        m.then_inc(bv_part, 1)

                    def b_turn(c):
                        pe.wait_ge(bv_copy, c + 1)
                        if c >= 2:
                            pe.wait_ge(bv_rows, c - 1)
                        for t in range(3):
                            m = pe.transpose(PS[:, 4 + c % 2, tile(t)], oT[:, tile(3 * c + t)], ident[:, :])
                        m.then_inc(bv_turned, 1)

                    for u in range(len(steps) + 2):
                        if u < len(steps):
                            b_scores(u)
                        if u >= 2:
                            b_values(u - 2)
                            if u - 2 in (12 + 5, 36 + 5):
                                b_turn(0 if u - 2 == 17 else 1)
                    b_turn(2)

                    pe.wait_ge(o_split, 2)
                    turn3(lambda t: hi_lo[:, t, :, :].rearrange("p a c -> p (a c)"), o_turned)
                    for t in range(NT):
                        pe.wait_ge(o_cols, t // 3 + 1)
                        m = both(PS[:, 3 + t // 2, 256 * (t % 2):256 * (t % 2) + 256], (fT[:, tile(t)],) * 2,
                                 (wo_s[:, 0, :], wo_s[:, 1, :]))
                        if t % 2 or t == NT - 1:
                            m.then_inc(o_proj, 1)

                    pe.wait_ge(f_split, 2)
                    turn3(lambda t: hi_lo[:, t, :, :].rearrange("p a c -> p (a c)"), f_turned)
                    for t in range(NT):
                        pe.wait_ge(f_cols, t // 3 + 1)
                        m = both(PS[:, 3 + t // 2, 256 * (t % 2):256 * (t % 2) + 256], (fT[:, tile(t)],) * 2,
                                 (rw_s[:, 0, :], rw_s[:, 1, :]))
                        if t % 2 or t == NT - 1:
                            m.then_inc(r_proj, 1)
                    pe.wait_ge(w_split, 2)
                    for t in range(NT):
                        m = pe.transpose(PS[0:16, t // 3, tile(t % 3)], wp[:, t, :], ident[:, :])
                        if t % 3 == 2:
                            m.then_inc(w_turned, 1)

                    def e_in(u):
                        c, g = u // NG, u % NG
                        if g == 0:
                            pe.wait_ge(w_cols, NC3)
                        if u >= 2:
                            pe.wait_ge(e_hid, u - 1)
                        k, gs = 3 * (u % 2), slice(g * P, g * P + GW[g])
                        fc = (fT[:, cols(c)],) * 2
                        both(PS[0:GW[g], k, 0:CW], (w1_s[:, 0, gs], w1_s[:, 1, gs]), fc)
                        both(PS[0:GW[g], k + 1, 0:CW], (w3_s[:, 0, gs], w3_s[:, 1, gs]), fc)
                        pe.matmul(PS[0:GW[g], k + 2, 0:CW], sel[:, gs], wT[:, cols(c)], start=True, stop=True)\
                            .then_inc(e_sum, 1)

                    def e_down(u):
                        c, g = u // NG, u % NG
                        pe.wait_ge(e_hid, u + 1)
                        if g == 0 and c == 2:
                            pe.wait_ge(e_rows, 1)
                        m = pe.matmul(PS[0:C, 6 + c % 2, 0:CW], w2_s[0:GW[g], g, :], hid[0:GW[g], u % 2, :],
                                      start=(g == 0), stop=(g == NG - 1)).then_inc(e_part, 1)

                    def e_turn(c):
                        pe.wait_ge(e_copy, c + 1)
                        for t in range(3):
                            m = pe.transpose(PS[:, 6 + c % 2, C * t:C * t + C], oT[0:C, tile(3 * c + t)], ident[0:C, 0:C])
                        m.then_inc(e_turned, 1)

                    for u in range(3 * NG + 1):
                        if u < 3 * NG:
                            e_in(u)
                        if u >= 1:
                            e_down(u - 1)
                            if u - 1 in (NG + 3, 2 * NG - 1 + 3):
                                pass
                            if (u - 1) % NG == 3 and u - 1 > NG:
                                e_turn((u - 1) // NG - 1)
                    e_turn(2)

                @block.scalar
                def _(act):
                    def out3(dst, counted, turned, part=P):
                        for c in range(NC3):
                            act.wait_ge(turned, c + 1)
                            act.activation(dst(c), PS[0:part, c, 0:CW], ACT.Copy).then_inc(counted, 1)

                    for c in range(2):
                        act.wait_ge(x_turned, c + 1)
                        act.activation(fT[:, c * HALF:(c + 1) * HALF], PS[:, c, :], ACT.Copy).then_inc(x_cols, 1)
                    for c in range(2):
                        cs = slice(c * HALF, (c + 1) * HALF)
                        act.wait_ge(k_sum, c + 1)
                        act.activation(ka[:, cs], PS[:, 4 + c, :], ACT.Identity, bias=bk_c[:, 0:1]).then_inc(k_hi, 1)
                        act.wait_ge(q_sum, c + 1)
                        act.activation(qa[:, cs], PS[:, 2 + c, :], ACT.Identity, bias=bq_c[:, 0:1]).then_inc(q_hi, 1)
                    for c in range(2):
                        cs = slice(c * HALF, (c + 1) * HALF)
                        act.wait_ge(mixed, NTI * (c + 1))
                        act.activation(yT[:, cs], PS[0:C, 6 + c, :], ACT.Relu, bias=bo_c[:, 0:1]).then_inc(y_parts, 1)
                        act.activation(neg[:, cs], PS[0:C, 6 + c, :], ACT.Relu, bias=nbo_c[:, 0:1], scale=-1.0)\
                            .then_inc(y_parts, 1)
                    act.wait_ge(y_turned, 1)
                    act.activation(H[:, 0:NTI, :], PS[:, 0, :].rearrange("p (t c) -> p t c", t=NTI), ACT.Copy)\
                        .then_inc(h_rows, 1)

                    out3(lambda c: ka[:, cols(c)], a_cols, a_turned)
                    for c in range(NC3):
                        act.wait_ge(aq_sum, c + 1)
                        act.activation(qa[:, cols(c)], PS[:, 3 + c, 0:CW], ACT.Copy).then_inc(aq_hi, 1)
                    for c in range(NC3):
                        act.wait_ge(am_turned, c + 1)
                        act.activation(qb[64:66, cols(c)], PS[64:66, 6, 0:CW], ACT.Copy).then_inc(am_rows, 1)
                    for n in range(3 * NT):
                        c, jt = n // NT, n % NT
                        act.wait_ge(at_sum, n + 1)
                        if n >= 4:
                            act.wait_ge(av_part, n - 3)
                        k = KEYS[jt]
                        act.activation(ring[0:k, n % 4, 0:CW], PS[0:k, n % 4, 0:CW], ACT.Exp, scale=C ** -0.5)\
                            .then_inc(at_exp, 1)
                        if (jt == 3 and c >= 1) or n == 3 * NT - 1:
                            d = c if n == 3 * NT - 1 else c - 1
                            act.wait_ge(av_part, NT * (d + 1))
                            act.activation(oT[0:66, cols(d)], PS[0:66, 4 + d % 2, 0:CW], ACT.Copy).then_inc(av_copy, 1)

                    out3(lambda c: fT[:, cols(c)], b_cols, b_turned)
                    for i in range(5):
                        m = min(2, NT - 2 * i)
                        act.wait_ge(b_rope, 2 * (i + 1))
                        act.activation(vv[:, 2 * i:2 * i + m, :, 0:HD],
                                       PS[:, 3 + i, 0:256 * m].rearrange("p (t n) -> p t n", t=m)[:, :, 96:128]
                                       .rearrange("p t (k d) -> p t k d", k=NKV), ACT.Copy).then_inc(b_v, 1)
                    for u in range(15):
                        n, c = u // 3, u % 3
                        act.wait_ge(bt_turned, u + 1)
                        dst = ka[:, cols(c)] if n == 0 else qT[:, n - 1, cols(c)]
                        act.activation(dst, PS[:, u % 3, 0:CW], ACT.Copy).then_inc(bt_cols, 1)
                    for u in range(3 * NH):
                        n, c = u // 3, u % 3
                        act.wait_ge(bm_turned, u + 1)
                        act.activation(qT[96:98, n, cols(c)], PS[96:98, 6 + u % 2, 0:CW], ACT.Copy).then_inc(bm_rows, 1)
                    steps = [(c, n, jt) for c in range(3) for n in range(NH) for jt in range(3 * c + 3)]
                    chunk_end = [12, 36, 72]
                    for u, (c, n, jt) in enumerate(steps):
                        act.wait_ge(bx_sum, u + 1)
                        if u >= 4:
                            act.wait_ge(bv_part, u - 3)
                        k = KEYS[jt]
                        keep, _ = kept(c, jt)
                        act.activation(ring[0:k, u % 4, keep:CW], PS[0:k, u % 4, keep:CW], ACT.Exp, scale=HD ** -0.5)\
                            .then_inc(bx_exp, 1)
                        if u in (12 + 4, 36 + 4, 71):
                            d = (16, 40, 71).index(u)
                            act.wait_ge(bv_part, chunk_end[d])
                            act.activation(oT[:, cols(d)], PS[:, 6 + d % 2, 0:CW], ACT.Copy).then_inc(bv_copy, 1)

                    out3(lambda c: fT[:, cols(c)], o_cols, o_turned)
                    out3(lambda c: fT[:, cols(c)], f_cols, f_turned)
                    act.wait_ge(r_in, 1)
                    act.activation(pr[:, :, :], lg[:, :, :], ACT.Exp).then_inc(r_exp, 1)
                    out3(lambda c: wT[:, cols(c)], w_cols, w_turned, part=16)
                    for u in range(3 * NG):
                        c, g = u // NG, u % NG
                        act.wait_ge(e_sum, u + 1)
                        if u >= 2:
                            act.wait_ge(e_mul, u - 1)
                        act.activation(ring[0:GW[g], u % 2, 0:CW], PS[0:GW[g], 3 * (u % 2), 0:CW], ACT.Silu)\
                            .then_inc(e_silu, 1)
                        if (g == 2 and c >= 1) or u == 3 * NG - 1:
                            d = c if u == 3 * NG - 1 else c - 1
                            act.wait_ge(e_part, NG * (d + 1))
                            act.activation(oT[0:C, cols(d)], PS[0:C, 6 + d % 2, 0:CW], ACT.Copy).then_inc(e_copy, 1)

                @block.vector
                def _(dve):
                    chain = [0]

                    def link(ins):
                        chain[0] += 1
                        ins.then_inc(dve_step, 1)
                        dve.wait_ge(dve_step, chain[0])

                    def split(src, counted):
                        h, low = hi_lo[:, 0:src.shape[1], 0, :], hi_lo[:, 0:src.shape[1], 1, :]
                        dve.tensor_copy(r(h), src).then_inc(counted, 1)
                        dve.wait_ge(counted, 1)
                        dve.tensor_tensor(r(low), src, h, ALU.subtract).then_inc(counted, 1)

                    def centre(src):
                        link(dve.tensor_reduce(st[:, 0, :], src, AX.X, ALU.add))
                        link(dve.tensor_scalar(st[:, 4, :], st[:, 0, :], -1.0 / C, None, ALU.mult))
                        link(dve.tensor_tensor(xc[:, :, :], src, spread(st[:, 4, :], C), ALU.add))

                    def squares(src):
                        link(dve.tensor_tensor(sq[:, :, :], src, src, ALU.mult))
                        dve.tensor_reduce(st[:, 1, :], sq[:, :, :], AX.X, ALU.add).then_inc(norm_sum, 1)

                    dve.wait_ge(x_in, 32)
                    split(xin[:, :, :], x_split)
                    for c in range(2):
                        cs = slice(c * HALF, (c + 1) * HALF)
                        dve.wait_ge(k_hi, c + 1)
                        dve.scalar_tensor_tensor(ka[64:128, cs], PS[64:128, 4 + c, :], bk_c[64:128, 0:1],
                                                 f(ka[64:128, cs]), ALU.add, ALU.subtract).then_inc(k_lo, 1)
                        dve.wait_ge(q_hi, c + 1)
                        dve.scalar_tensor_tensor(qb[:, cs], PS[:, 2 + c, :], bq_c[:, 0:1], f(qa[:, cs]),
                                                 ALU.add, ALU.subtract).then_inc(q_lo, 1)
                    for i in range(4):
                        dve.wait_ge(v_sum, i + 1)
                        dve.tensor_tensor(vt[:, 2 * i:2 * i + 2, :],
                                          PS[:, (6, 7, 0, 1)[i], :].rearrange("p (t n) -> p t n", t=2)[:, :, 0:C],
                                          every(bv_row[:, :], 2), ALU.add).then_inc(v_out, 1)
                    for n in range(2 * NTI):
                        c, s = n // NTI, n % NTI
                        dve.wait_ge(ts_sum, n + 1)
                        if n >= 4:
                            dve.wait_ge(mixed, n - 3)
                        dve.tensor_tensor(ring[:, n % 4, :], PS[:, 2 + n % 4, :], gT[:, s, c * HALF:(c + 1) * HALF],
                                          ALU.mult).then_inc(gated, 1)
                    for c in range(2):
                        cs = slice(c * HALF, (c + 1) * HALF)
                        dve.wait_ge(y_parts, 2 * (c + 1))
                        dve.scalar_tensor_tensor(yT[:, cs], neg[:, cs], na_c[:, 0:1], yT[:, cs], ALU.mult, ALU.add)\
                            .then_inc(y_cols, 1)

                    dve.wait_ge(h_rows, 1)
                    centre(H[:, :, :])
                    squares(xc[:, :, :])
                    dve.wait_ge(norm_root, 1)
                    link(dve.tensor_tensor(xv[:, :, 0:C], xc[:, :, :], spread(st[:, 3, :], C), ALU.mult))
                    split(xv[:, :, 0:C], a_split)
                    dve.wait_ge(a_cols, NC3)
                    dve.tensor_copy(xb[0:C, :], f(ka[0:C, :])).then_inc(a_copy, 1)
                    for c in range(NC3):
                        dve.wait_ge(aq_hi, c + 1)
                        dve.tensor_tensor(qb[0:C, cols(c)], PS[0:C, 3 + c, 0:CW], f(qa[0:C, cols(c)]), ALU.subtract)\
                            .then_inc(aq_lo, 1)
                    for t in range(NT):
                        dve.wait_ge(as_sum, t + 1)
                        k = 3 * (t % 2)
                        dve.tensor_reduce(nm[:, t:t + 1], PS[:, k:k + 3, 0:JW], AX.XY, ALU.max, negate=True)\
                            .then_inc(as_max, 1)
                        if t % 3 == 2:
                            ts = slice(t - 2, t + 1)
                            dve.wait_ge(as_max, t + 1)
                            link(dve.tensor_copy(r(mp[:, ts, 64:65]), nm[:, ts].unsqueeze(2)))
                            dve.tensor_tensor(r(mp[:, ts, 65:66]), nm[:, ts].unsqueeze(2), mp[:, ts, 64:65], ALU.subtract)\
                                .then_inc(am_split, 1)
                    for c in range(NC3):
                        cs = slice(3 * c, 3 * c + 3)
                        dve.wait_ge(av_turned, c + 1)
                        o = PS[:, 7, 0:3 * 66].rearrange("p (t n) -> p t n", t=3)
                        link(dve.reciprocal(rden[:, cs, 0:1], o[:, :, 64:65]))
                        dve.tensor_tensor(sq[:, cs, :], o[:, :, 0:C], rden[:, cs, 0:1].broadcast_to([P, 3, C]), ALU.mult)\
                            .then_inc(av_rows, 1)
                        dve.wait_ge(av_rows, c + 1)
                        link(dve.tensor_tensor(H2[:, cs, :], H[:, cs, :], sq[:, cs, :], ALU.add))

                    centre(H2[:, :, :])
                    squares(xc[:, :, :])
                    dve.wait_ge(norm_root, 2)
                    link(dve.tensor_tensor(Y[:, :, :], xc[:, :, :], spread(st[:, 3, :], C), ALU.mult))
                    squares(Y[:, :, :])
                    link(dve.tensor_tensor(xc[:, :, :], Y[:, :, :], every(ln1_b[:, :], NT), ALU.mult))
                    dve.wait_ge(norm_root, 3)
                    link(dve.tensor_tensor(hn[:, :, :], xc[:, :, :], spread(st[:, 3, :], C), ALU.mult))
                    split(hn[:, :, :], b_split)
                    for i in range(5):
                        m = min(2, NT - 2 * i)
                        ts = slice(2 * i, 2 * i + m)
                        dve.wait_ge(b_proj, i + 1)
                        o = PS[:, 3 + i, 0:256 * m].rearrange("p (t n) -> p t n", t=m)
                        for k, table in ((0, cos), (1, sin)):
                            dve.tensor_tensor(rot[:, k, ts, :].rearrange("p t (h d) -> p t h d", h=6),
                                              o[:, :, P * k:P * k + 96].rearrange("p t (h d) -> p t h d", h=6),
                                              table[:, ts, :].unsqueeze(2).broadcast_to([P, m, 6, HD]), ALU.mult)\
                                .then_inc(b_rope, 1)
                    dve.wait_ge(b_rope, 10)
                    link(dve.tensor_tensor(qk[:, :, :], rot[:, 0, :, :], rot[:, 1, :, :], ALU.add))
                    dve.tensor_copy(r(qkh[:, :, :]), qk[:, :, :]).then_inc(b_qk, 1)
                    dve.wait_ge(b_qk, 1)
                    dve.tensor_tensor(r(qkl[:, :, :]), qk[:, :, :], qkh[:, :, :], ALU.subtract).then_inc(b_qk, 1)
                    for n in range(NH):
                        o = HD * (n // 2)
                        src = qkh[:, :, n * HD:(n + 1) * HD].unsqueeze(2).broadcast_to([P, NT, 2, HD])
                        dve.tensor_copy(qp[:, :, n, 0:2, o:o + HD], src).then_inc(b_slot_dve, 1)
                    for n in range(NH):
                        for t in range(NT):
                            u = NT * n + t
                            count, wide = CHUNKS[t]
                            dve.wait_ge(bs_sum, u + 1)
                            k = 3 * (u % 2)
                            src = PS[:, k:k + count, 0:wide] if t else PS[:, k:k + 1, 0:P]
                            dve.tensor_reduce(nm4[:, n, t:t + 1], src, AX.XY, ALU.max, negate=True).then_inc(bs_max, 1)
                        dve.wait_ge(bs_max, NT * (n + 1))
                        m4 = nm4[:, n, :].unsqueeze(2)
                        link(dve.tensor_copy(r(qp[:, :, n, 3, 0:1]), m4))
                        dve.tensor_tensor(r(qp[:, :, n, 3, 1:2]), m4, qp[:, :, n, 3, 0:1], ALU.subtract).then_inc(bm_split, 1)
                    for c in range(NC3):
                        cs = slice(3 * c, 3 * c + 3)
                        dve.wait_ge(bv_turned, c + 1)
                        o = PS[:, 4 + c % 2, 0:CW].rearrange("p (t h d) -> p t h d", t=3, h=NH)
                        link(dve.reciprocal(rden[:, cs, :].unsqueeze(3), o[:, :, :, 16:17]))
                        dve.tensor_tensor(hn[:, cs, :].rearrange("p t (h d) -> p t h d", h=NH), o[:, :, :, 0:HD],
                                          rden[:, cs, :].unsqueeze(3).broadcast_to([P, 3, NH, HD]), ALU.mult)\
                            .then_inc(bv_rows, 1)
                    dve.wait_ge(bv_rows, NC3)
                    split(hn[:, :, :], o_split)
                    for i in range(5):
                        m = min(2, NT - 2 * i)
                        ts = slice(2 * i, 2 * i + m)
                        dve.wait_ge(o_proj, i + 1)
                        o = PS[:, 3 + i, 0:256 * m].rearrange("p (t n) -> p t n", t=m)
                        dve.tensor_tensor(R1[:, ts, :], o[:, :, 0:C], Y[:, ts, :], ALU.add).then_inc(o_rows, 1)
                    dve.wait_ge(o_rows, 5)
                    squares(R1[:, :, :])
                    link(dve.tensor_tensor(xc[:, :, :], R1[:, :, :], every(ln2_b[:, :], NT), ALU.mult))
                    dve.wait_ge(norm_root, 4)
                    link(dve.tensor_tensor(hn[:, :, :], xc[:, :, :], spread(st[:, 3, :], C), ALU.mult))
                    split(hn[:, :, :], f_split)
                    for i in range(5):
                        m = min(2, NT - 2 * i)
                        ts = slice(2 * i, 2 * i + m)
                        dve.wait_ge(r_proj, i + 1)
                        o = PS[:, 3 + i, 0:256 * m].rearrange("p (t n) -> p t n", t=m)
                        link(dve.tensor_copy(lg[:, ts, :], o[:, :, 0:NE]))
                    link(dve.tensor_reduce(st[:, 5, :], lg[:, :, :], AX.X, ALU.max))
                    dve.tensor_tensor(lg[:, :, :], lg[:, :, :], spread(st[:, 5, :], NE), ALU.subtract).then_inc(r_in, 1)
                    dve.wait_ge(r_exp, 1)
                    link(dve.tensor_reduce(st[:, 6, :], pr[:, :, :], AX.X, ALU.add))
                    link(dve.reciprocal(st[:, 7, :], st[:, 6, :]))
                    link(dve.tensor_tensor(pr[:, :, :], pr[:, :, :], spread(st[:, 7, :], NE), ALU.mult))
                    mine = pr[:, :, :].unsqueeze(3).broadcast_to([P, NT, NE, NE])
                    other = pr[:, :, :].unsqueeze(2).broadcast_to([P, NT, NE, NE])
                    c4 = [cmp[:, i, :, :].rearrange("p t (a b) -> p t a b", a=NE) for i in range(2)]
                    dve.tensor_tensor(c4[0], other, mine, ALU.is_gt)
                    link(dve.tensor_tensor(c4[1], other, mine, ALU.is_equal))
                    link(dve.tensor_tensor(cmp[:, 1, :, :], cmp[:, 1, :, :], every(tri[:, :], NT), ALU.mult))
                    link(dve.tensor_tensor(cmp[:, 0, :, :], cmp[:, 0, :, :], cmp[:, 1, :, :], ALU.add))
                    link(dve.tensor_reduce(wt[:, :, :], c4[0], AX.X, ALU.add))
                    link(dve.scalar_tensor_tensor(wt[:, :, :], wt[:, :, :], 1.5, pr[:, :, :], ALU.is_lt, ALU.mult))
                    link(dve.tensor_reduce(st[:, 5, :], wt[:, :, :], AX.X, ALU.add))
                    link(dve.tensor_scalar(st[:, 6, :], st[:, 5, :], 1e-9, None, ALU.add))
                    link(dve.reciprocal(st[:, 7, :], st[:, 6, :]))
                    link(dve.tensor_tensor(wt[:, :, :], wt[:, :, :], spread(st[:, 7, :], NE), ALU.mult))
                    dve.tensor_copy(r(wp[:, :, 0:NE]), wt[:, :, :]).then_inc(w_split, 1)
                    dve.wait_ge(w_split, 1)
                    dve.tensor_tensor(r(wp[:, :, NE:16]), wt[:, :, :], wp[:, :, 0:NE], ALU.subtract).then_inc(w_split, 1)
                    def e_result(c):
                        cs = slice(3 * c, 3 * c + 3)
                        dve.wait_ge(e_turned, c + 1)
                        dve.tensor_tensor(sq[:, cs, :], PS[:, 6 + c % 2, 0:3 * C].rearrange("p (t n) -> p t n", t=3),
                                          H[:, cs, :], ALU.add).then_inc(e_rows, 1)

                    dve.wait_ge(hr_done, 1)
                    for u in range(3 * NG):
                        c, g = u // NG, u % NG
                        k = 3 * (u % 2)
                        gw = GW[g]
                        dve.wait_ge(e_silu, u + 1)
                        dve.tensor_tensor(ring[0:gw, 2 + u % 2, 0:CW], PS[0:gw, k + 1, 0:CW], ring[0:gw, u % 2, 0:CW],
                                          ALU.mult).then_inc(e_mul, 1)
                        dve.wait_ge(e_mul, u + 1)
                        if u >= 2:
                            dve.wait_ge(e_part, u - 1)
                        dve.tensor_tensor(hid[0:gw, u % 2, :], PS[0:gw, k + 2, 0:CW], ring[0:gw, 2 + u % 2, 0:CW],
                                          ALU.mult).then_inc(e_hid, 1)
                        if g == 5 and c >= 1:
                            e_result(c - 1)
                    e_result(2)

            nc.all_engine_barrier(sems_to_clear=range(min(loop_sems), max(loop_sems) + 1))


_INS = ['x', 'txt', 'L0_tok_d_gamma_batched', 'L0_tok_Wq', 'L0_tok_bq', 'L0_tok_Wk', 'L0_tok_bk', 'L0_tok_Wv',
        'L0_tok_bv', 'L0_tok_Wo', 'L0_tok_bo', 'L0_tok_prelu_a', 'L0_attn_Wq', 'L0_attn_Wk', 'L0_ffn_ln1_w',
        'L0_ffn_ln2_w', 'L0_ffn_wq', 'L0_ffn_wk', 'L0_ffn_wv', 'L0_ffn_wo', 'L0_ffn_router_w', 'L0_ffn_w1',
        'L0_ffn_w2', 'L0_ffn_w3']


def _constants():
    import numpy as np

    i = np.arange(P)
    above = np.where(i[None, :] > i[:, None], np.float32(-1e30), np.float32(0))
    inv_freq = 1.0 / 10000.0 ** (np.arange(0, HD, 2, dtype=np.float32) / HD)
    freqs = np.outer(np.arange(TP, dtype=np.float32), inv_freq.astype(np.float32))
    emb = np.concatenate([freqs, freqs], axis=-1)
    table = lambda a: np.ascontiguousarray(a.astype(np.float32).reshape(NT, P, HD).transpose(1, 0, 2))
    owner = np.arange(NG * P) // HID
    sel = (owner[None, :] == (np.arange(16) % NE)[:, None]).astype(np.float32)
    e = np.arange(NE)
    tri = np.tile((e[None, :] < e[:, None]).astype(np.float32).reshape(1, -1), (P, 1))
    return {
        "c_ident": np.eye(P, dtype=np.float32),
        "c_mask": np.ascontiguousarray(np.stack([above, above.T], axis=1)),
        "c_cos": table(np.cos(emb)),
        "c_sin": table(np.sin(emb)),
        "c_sel": sel,
        "c_tri": tri,
    }


def kernel(**inputs):
    import numpy as np
    import concourse.bacc as bacc
    from concourse.bass_utils import run_bass_kernel_spmd

    nc = bacc.Bacc("TRN2", target_bir_lowering=False, num_devices=1)
    arrays, args = {}, []
    given = {n: np.asarray(inputs[n]) for n in _INS}
    given['L0_tok_prelu_a'] = given['L0_tok_prelu_a'].reshape(1, 1)
    given.update(_constants())
    for name, a in given.items():
        a = np.ascontiguousarray(a)
        arrays[f"in_{name}"] = a
        args.append(nc.dram_tensor(f"in_{name}", a.shape, mybir.dt.from_np(a.dtype), kind="ExternalInput").ap())
    args.append(nc.dram_tensor("out_0", (B, T, C), F32, kind="ExternalOutput").ap())
    early_fusion_kernel(nc, *args)
    res = run_bass_kernel_spmd(nc, [arrays], core_ids=[0])
    return res.results[0]["out_0"]
```

```python
import concourse.bass as bass
from concourse import mybir
from contextlib import ExitStack

F32 = mybir.dt.float32
FR = mybir.dt.float32r
BF = mybir.dt.bfloat16
ALU = mybir.AluOpType
ACT = mybir.ActivationFunctionType
AX = mybir.AxisListType

P = 128
B, T_IMG, C = 8, 1024, 64
T_TXT = 77
T = T_IMG + T_TXT
NT = 9
TP = NT * P
NTI = T_IMG // P
LAST = T - NTI * P
HALF = 512
NC3 = 3
CW = 3 * P
JW = T // 3
NH, NKV, HD = 4, 2, 16
NE, HID = 8, 170
FH = NE * HID
NG = (FH + P - 1) // P
GW = [min(P, FH - P * g) for g in range(NG)]
KEYS = [P] * NTI + [LAST]
LN_EPS, RMS_EPS = 1e-5, 1e-6
CHUNKS = [(1, 256), (1, 256), (1, 384), (1, 512), (2, 320), (2, 384), (2, 448), (2, 512), (3, 368)]


def early_fusion_kernel(nc, x, txt, gamma, tWq, tbq, tWk, tbk, tWv, tbv, tWo, tbo, prelu_a, aWq, aWk,
                        ln1_w, ln2_w, wq, wk, wv, wo, router_w, w1, w2, w3,
                        c_ident, c_mask, c_cos, c_sin, c_sel, c_tri, out):
    ctx = ExitStack()
    with ctx:
        def sb(name, shape, dt=F32):
            return ctx.enter_context(nc.sbuf_tensor(name, shape, dt))

        sem_nums = []

        def sem(name):
            s = ctx.enter_context(nc.semaphore(name))
            sem_nums.append(s.num)
            return s

        def f(ap):
            return ap.bitcast(F32)

        def r(ap):
            return ap.bitcast(FR)

        def spread(ap, n):
            return ap.unsqueeze(2).broadcast_to([ap.shape[0], ap.shape[1], n])

        def every(ap, n):
            return ap.unsqueeze(1).broadcast_to([ap.shape[0], n, ap.shape[1]])

        ident = sb("ident", [P, P])
        identb = sb("identb", [P, P], BF)
        maskb = sb("maskb", [P, 2, P], BF)
        cos = sb("cos", [P, NT, HD])
        sin = sb("sin", [P, NT, HD])
        tri = sb("tri", [P, NE * NE])
        sel = sb("sel", [P, NG * P], FR)
        gT = sb("gT", [P, NTI, T_IMG])
        bq_c = sb("bq_c", [P, 1])
        bk_c = sb("bk_c", [P, 1])
        bv_c = sb("bv_c", [C, 1])
        a_c = sb("a_c", [P, 1])
        bo_row = sb("bo_row", [P, C])
        nhalf = sb("nhalf", [P, 1])
        bv_row = sb("bv_row", [P, C])
        ln1_b = sb("ln1_b", [P, C])
        ln2_b = sb("ln2_b", [P, C])
        tq_s = sb("tq_s", [P, 2, P], FR)
        tk_s = sb("tk_s", [P, 2, P], FR)
        side_s = sb("side_s", [P, 2, CW], FR)
        vo_s, wo_s, rw_s = (side_s[:, :, C * i:C * i + 256] for i in range(3))
        a_s = sb("a_s", [P, 2, P], FR)
        qkv_s = sb("qkv_s", [P, 2, 256], FR)
        w1_s = sb("w1_s", [P, 2, NG * P], FR)
        w3_s = sb("w3_s", [P, 2, NG * P], FR)
        w2_s = sb("w2_s", [P, NG, C])
        fold = sb("fold", [P, C])
        ones = sb("ones", [P, 1])

        class Region:
            def __init__(self, tensor, at):
                self.tensor, self.at = tensor, at

            def take(self, parts, *shape):
                n = 1
                for d in shape:
                    n *= d
                ap = self.tensor[0:parts, self.at:self.at + n]
                self.at += n
                if len(shape) == 2:
                    return ap.rearrange("p (a b) -> p a b", b=shape[1])
                if len(shape) == 3:
                    return ap.rearrange("p (a b c) -> p a b c", b=shape[1], c=shape[2])
                return ap

        region = sb("region", [P, 4320])
        prep = Region(region, 0)
        maskf = prep.take(P, 2, P)
        stage = prep.take(P, 6, P)
        wstage = prep.take(P, NG, 2, C)
        w2stage = prep.take(C, FH)
        qkv_f = prep.take(P, 256)
        mixing = Region(region, 0)
        yT = mixing.take(P, T_IMG)
        xin = mixing.take(P, NTI, C)
        vt = mixing.take(P, NTI, C)
        first = Region(region, 0)
        oT = first.take(P, TP)
        sums = first.take(P, 2, CW)
        rest = Region(region, 0)
        rot = rest.take(P, 2, NT, 96)
        qk = rest.take(P, NT, 96)
        hn = rest.take(P, NT, C)
        sq = rest.take(P, NT, C)
        xc = rest.take(P, NT, C)

        hi_lo = sb("hi_lo", [P, NT, 2, C])
        qa = sb("qa", [P, TP], FR)
        qb = sb("qb", [P, TP], FR)
        ka = sb("ka", [P, TP], FR)
        xb = sb("xb", [P, TP], FR)
        ring = sb("ring", [P, 5, HALF])
        H = sb("H", [P, NT, C])
        H2 = sb("H2", [P, NT, C])
        Y = sb("Y", [P, NT, C])
        st = sb("st", [P, 5, NT])
        xv = sb("xv", [P, NT, C])
        nmp = sb("nmp", [P, NT, 3])
        nm = sb("nm", [P, NT])
        rden = sb("rden", [P, NT, 1])
        qp = sb("qp", [P, NT, 2, 4, 32])
        kp = sb("kp", [P, NT, NKV, 4, 32])
        g_row = qp[:, :, :, :, :].rearrange("p t a b c -> p (t a b c)")[:, 0:2 * T_IMG]\
            .rearrange("p (a b) -> p a b", a=2)
        mp = qp[:, :, 0, 0:3, :].rearrange("p t a b -> p t (a b)")
        qT = sb("qT", [P, 2, TP], FR)
        kT = sb("kT", [P, NKV, TP], FR)
        vv = sb("vv", [P, NT, NKV, 32])
        H2y = sb("H2y", [P, NT, C])
        hi_lo_y = sb("hi_lo_y", [P, NT, 2, C], FR)
        wT = hi_lo_y[:, :, :, :].rearrange("p t a c -> p (t a c)")
        fT = sb("fT", [P, TP], FR)
        ring_y = sb("ring_y", [P, 8, CW])
        sel_f = ring_y[0:16, :, :].rearrange("p a b -> p (a b)")[:, 0:NG * P]
        hid = ring_y[:, 4:8, :]
        sty = sb("sty", [P, 8, NT])
        rden_y = sb("rden_y", [P, NT, NH])
        nm4 = sb("nm4", [P, NH, NT])
        nmp_y = sb("nmp_y", [P, NT, 3])
        hn_y = sb("hn_y", [P, NT, C])
        mp4 = hn_y[:, :, :].rearrange("p t (a b) -> p t a b", a=2)
        R1 = sb("R1", [P, NT, C])
        pair_y = sb("pair_y", [P, 2, NT, C])
        xc_y, sq_y = pair_y[:, 0, :, :], pair_y[:, 1, :, :]
        cmp = pair_y
        oT_y = pair_y[:, :, :, :].rearrange("p a t c -> p (a t c)")
        lg = sb("lg", [P, NT, NE])
        pr = sb("pr", [P, NT, NE])
        wt = sb("wt", [P, NT, NE])
        wp = sb("wp", [P, NT, 16])

        PS = ctx.enter_context(nc.psum_tensor("PS", [P, 8, HALF], F32))

        p_id = sem("p_id")
        p_w = sem("p_w")
        p_in = sem("p_in")
        p_g = [sem("p_g0"), sem("p_g1")]
        p_set = sem("p_set")
        p_pe = sem("p_pe")
        p_dv = sem("p_dv")
        p_gt = sem("p_gt")
        p_gc = sem("p_gc")
        NIN = [0]
        ROW_BANKS = [[0, 1, 2], [3, 6, 7]]

        def load_rows(queue, w):
            rows = w.rearrange("e k c -> (e k) c")
            for h in range(2):
                queue.dma_start(wstage[:, 0:NG - 1, h, :],
                             rows[0:(NG - 1) * P, :].rearrange("(g p) c -> p g c", p=P)).then_inc(p_w, 16)
                queue.dma_start(wstage[0:GW[-1], NG - 1, h, :], rows[(NG - 1) * P:FH, :]).then_inc(p_w, 16)

        with nc.Block() as block:
            @block.sync
            def _(sp):
                def load(dst, src):
                    sp.dma_start(dst, src).then_inc(p_in, 16)
                    NIN[0] += 1

                sp.dma_start(ident[:, :], c_ident).then_inc(p_id, 16)
                load_rows(sp, w1)
                load(maskf, c_mask)
                load(cos[:, :, :], c_cos)
                load(sin[:, :, :], c_sin)
                load(sel_f, c_sel)
                load(tri[:, :], c_tri)
                col = lambda v: v.rearrange("(n a) -> n a", a=1)
                row = lambda v: v.rearrange("(a n) -> a n", a=1)
                for h in range(2):
                    hs = slice(C * h, C * h + C)
                    load(bq_c[hs, :], col(tbq))
                    load(bk_c[hs, :], col(tbk))
                    load(stage[hs, 0, 0:C], tWq)
                    load(stage[hs, 1, 0:C], tWk)
                    load(stage[0:64, 3, hs], wq)
                    load(stage[64:96, 3, hs], wk)
                    load(stage[96:128, 3, hs], wv)
                    load(stage[0:C, 4, hs], wo)
                    load(stage[0:NE, 5, hs], router_w)
                load(bv_c[:, :], col(tbv))
                load(bo_row[:, :], row(tbo).broadcast_to([P, C]))
                load(a_c[:, :], prelu_a.broadcast_to([P, 1]))
                load(ln1_b[:, :], row(ln1_w).broadcast_to([P, C]))
                load(ln2_b[:, :], row(ln2_w).broadcast_to([P, C]))
                load(stage[0:C, 2, 0:C], tWv)
                load(stage[0:C, 2, C:P], tWo)
                load(ring[0:C, 0, 0:C], aWq)
                load(ring[0:C, 0, C:P], aWk)
                load(w2stage[:, :].rearrange("c (e k) -> c e k", e=NE), w2.rearrange("e c k -> c e k"))
            @block.gpsimd
            def _(pool):
                for m in (H, H2, hi_lo, xv, kp, vv, wp):
                    flat = m[:]
                    pool.memset(flat, 0.0).then_inc(p_set, 1)
                pool.memset(f(side_s[:, :, :]), 0.0).then_inc(p_set, 1)
                pool.memset(f(sel[:, :]), 0.0).then_inc(p_set, 1)
                pool.memset(f(xb[:, :]), 0.0).then_inc(p_set, 1)
                pool.memset(qkv_f, 0.0).then_inc(p_set, 1)
                pool.memset(nhalf[:, :], -0.5).then_inc(p_set, 1)
                pool.memset(qp[:, NT - 1, :, :, :], 0.0).then_inc(p_set, 1)
                pool.wait_ge(p_set, 13)
                pool.memset(f(xb[64:66, :]), 1.0).then_inc(p_set, 1)
                pool.wait_ge(p_set, 14)
                pool.memset(ones[:, :], 1.0).then_inc(p_set, 1)
                for g in range(NKV):
                    pool.memset(kp[:, :, g, 3, 2 * g:2 * g + 2], 1.0).then_inc(p_set, 1)
                pool.memset(vv[:, :, :, 16:17], 1.0).then_inc(p_set, 1)
                pool.wait_ge(p_gt, 2 * NTI)
                pool.memset(qp[:, :, :, 3, :], 0.0).then_inc(p_set, 1)
                pool.memset(hn_y[:, :, :], 0.0).then_inc(p_set, 1)

            @block.tensor
            def _(pe):
                def rows_T(n):
                    pe.wait_ge(p_w, 64 * (n + 1))
                    for g in range(NG):
                        m = pe.transpose(PS[:, ROW_BANKS[n][g // 4], (g % 4) * P:(g % 4) * P + GW[g]],
                                         wstage[0:GW[g], g, :, :].rearrange("p a c -> p (a c)"),
                                         ident[0:GW[g], 0:GW[g]])
                    m.then_inc(p_pe, 1)

                def gates_T(tiles):
                    for t in tiles:
                        pe.wait_ge(p_g[t % 2], 16 * (t // 2 + 1))
                        for h in range(2):
                            n = 2 * t + h
                            if n >= 2:
                                pe.wait_ge(p_gc, n - 1)
                            for s in range(4):
                                m = pe.transpose(PS[:, 4 + n % 2, s * P:(s + 1) * P],
                                                 g_row[:, t % 2, (4 * h + s) * P:(4 * h + s + 1) * P], ident[:, :])
                            m.then_inc(p_gt, 1)

                pe.wait_ge(p_id, 16)
                gates_T(range(0, 1))
                rows_T(0)
                gates_T(range(1, 4))
                rows_T(1)
                pe.wait_ge(p_in, 16 * NIN[0])
                pe.wait_ge(p_dv, 1)
                pe.transpose(PS[:, 0, 0:P], stage[:, 3, :], ident[:, :])
                pe.transpose(PS[:, 0, P:P + C], stage[0:C, 4, :], ident[0:C, 0:C])
                pe.transpose(PS[:, 0, 256:256 + NE], stage[0:NE, 5, :], ident[0:NE, 0:NE])
                pe.transpose(PS[0:C, 0, 384:384 + C], stage[0:C, 2, 0:C], ident[0:C, 0:C]).then_inc(p_pe, 1)
                gates_T(range(4, 6))
                pe.wait_ge(p_dv, 3)
                pe.matmul(PS[:, 1, 0:C], ring[0:C, 1, 0:P], stage[0:C, 2, C:P], start=True, stop=True)
                pe.matmul(PS[:, 1, C:P], ring[0:C, 1, P:2 * P], ring[0:C, 0, C:P], start=True, stop=True)
                pe.matmul(PS[:, 1, P:P + C], ring[0:C, 1, 256:384], stage[0:C, 2, C:P],
                          start=True, stop=True).then_inc(p_pe, 1)
                for g in range(NG):
                    m = pe.transpose(PS[0:GW[g], 2 + g // 8, (g % 8) * C:(g % 8) * C + C],
                                     w2stage[:, g * P:g * P + GW[g]], ident[0:C, 0:C])
                m.then_inc(p_pe, 1)
                gates_T(range(6, NTI))

            @block.vector
            def _(dve):
                chain = [0]
                p_ch = sem("p_ch")

                def link(ins):
                    chain[0] += 1
                    ins.then_inc(p_ch, 1)
                    dve.wait_ge(p_ch, chain[0])

                def split(dst, src):
                    h, low = dst
                    link(dve.tensor_copy(h, src))
                    return dve.tensor_tensor(low, src, f(h), ALU.subtract)

                for n, w in enumerate((w1_s, w3_s)):
                    dve.wait_ge(p_pe, n + 1)
                    for j, bank in enumerate(ROW_BANKS[n]):
                        cs = slice(HALF * j, min(HALF * (j + 1), FH))
                        last = split((w[:, 0, cs], w[:, 1, cs]), PS[:, bank, 0:cs.stop - cs.start])
                    last.then_inc(p_dv, 1)
                dve.wait_ge(p_set, 18)
                dve.wait_ge(p_in, 16 * NIN[0])
                dve.tensor_copy(identb[:, :], ident[:, :])
                dve.tensor_copy(maskb[:, :, :], maskf[:, :, :])
                dve.tensor_copy(sel[0:16, :], sel_f[:, :])
                dve.tensor_tensor(fold[:, :], ident[:, 0:C], ident[:, C:P], ALU.add)
                for w, k in ((tq_s, 0), (tk_s, 1)):
                    for h in range(2):
                        hs = slice(C * h, C * h + C)
                        split((w[:, 0, hs], w[:, 1, hs]), stage[:, k, 0:C])
                dve.wait_ge(p_pe, 3)
                dve.tensor_copy(qkv_f[:, 0:P], PS[:, 0, 0:P])
                src = PS[:, 0, 0:96].rearrange("p (h a b) -> p h a b", h=6, a=2)
                dst = qkv_f[:, P:P + 96].rearrange("p (h a b) -> p h a b", h=6, a=2)
                dve.tensor_scalar(dst[:, :, 0, :], src[:, :, 1, :], -1.0, None, ALU.mult)
                link(dve.tensor_copy(dst[:, :, 1, :], src[:, :, 0, :]))
                split((qkv_s[:, 0, :], qkv_s[:, 1, :]), qkv_f)
                split((wo_s[:, 0, 0:C], wo_s[:, 1, 0:C]), PS[:, 0, P:P + C])
                split((rw_s[:, 0, 0:NE], rw_s[:, 1, 0:NE]), PS[:, 0, 256:256 + NE])
                for h in range(2):
                    hs = slice(C * h, C * h + C)
                    dve.tensor_copy(ring[0:C, 1, hs], PS[0:C, 0, 384:384 + C])
                    dve.tensor_copy(ring[0:C, 1, P + C * h:P + C * h + C], ring[0:C, 0, 0:C])
                dve.tensor_copy(ring[0:C, 1, 256:384], bv_c[:, 0:1].broadcast_to([C, P])).then_inc(p_dv, 1)
                dve.wait_ge(p_pe, 4)
                split((vo_s[:, 0, 0:C], vo_s[:, 1, 0:C]), PS[:, 1, 0:C])
                for h in range(2):
                    hs = slice(C * h, C * h + C)
                    split((a_s[:, 0, hs], a_s[:, 1, hs]), PS[:, 1, C:P])
                dve.tensor_copy(bv_row[:, :], PS[:, 1, P:P + C])
                dve.wait_ge(p_pe, 5)
                dve.tensor_copy(w2_s[:, 0:8, :], PS[:, 2, :].rearrange("p (g c) -> p g c", g=8))
                dve.tensor_copy(w2_s[:, 8:10, :], PS[:, 3, 0:2 * C].rearrange("p (g c) -> p g c", g=2))
                dve.tensor_copy(w2_s[0:GW[-1], 10, :], PS[0:GW[-1], 3, 2 * C:3 * C])

            @block.scalar
            def _(act):
                for t in range(2):
                    act.dma_start(g_row[:, t, :], gamma[t * P:(t + 1) * P, :]).then_inc(p_g[t], 16)
                for n in range(2 * NTI):
                    t, h = n // 2, n % 2
                    if n == 4:
                        act.wait_ge(p_pe, 1)
                        load_rows(act, w3)
                    if h == 0 and 2 <= t + 1 < NTI:
                        act.wait_ge(p_gc, 2 * t)
                        act.dma_start(g_row[:, (t + 1) % 2, :], gamma[(t + 1) * P:(t + 2) * P, :])\
                            .then_inc(p_g[(t + 1) % 2], 16)
                    act.wait_ge(p_gt, n + 1)
                    act.activation(gT[:, 4 * h:4 * h + 4, t * P:(t + 1) * P],
                                   PS[:, 4 + n % 2, :].rearrange("p (s c) -> p s c", s=4), ACT.Copy).then_inc(p_gc, 1)

        first_loop_sem = len(sem_nums)
        x_in = sem("x_in")
        x_split = sem("x_split")
        x_turned = sem("x_turned")
        x_cols = sem("x_cols")
        kq_sum = sem("kq_sum")
        kq_hi = sem("kq_hi")
        kq_lo = sem("kq_lo")
        v_sum = sem("v_sum")
        v_out = sem("v_out")
        ts_sum = sem("ts_sum")
        moved = sem("moved")
        gated = sem("gated")
        mixed = sem("mixed")
        y_cols = sem("y_cols")
        y_turned = sem("y_turned")
        y_biased = sem("y_biased")
        h_rows = sem("h_rows")
        norm_sum = sem("norm_sum")
        norm_root = sem("norm_root")
        a_split = sem("a_split")
        a_turned = sem("a_turned")
        a_cols = sem("a_cols")
        a_ones = sem("a_ones")
        a_copy = sem("a_copy")
        aq_sum = sem("aq_sum")
        aq_hi = sem("aq_hi")
        aq_lo = sem("aq_lo")
        as_sum = sem("as_sum")
        as_max = sem("as_max")
        am_split = sem("am_split")
        am_turned = sem("am_turned")
        am_rows = sem("am_rows")
        at_sum = sem("at_sum")
        at_exp = sem("at_exp")
        at_added = sem("at_added")
        av_part = sem("av_part")
        av_copy = sem("av_copy")
        av_turned = sem("av_turned")
        av_rows = sem("av_rows")
        b_split = sem("b_split")
        b_turned = sem("b_turned")
        b_cols = sem("b_cols")
        b_proj = sem("b_proj")
        b_rope = sem("b_rope")
        b_v = sem("b_v")
        b_slot = sem("b_slot")
        bt_turned = sem("bt_turned")
        bt_cols = sem("bt_cols")
        bs_sum = sem("bs_sum")
        bs_max = sem("bs_max")
        bm_split = sem("bm_split")
        bm_turned = sem("bm_turned")
        bm_rows = sem("bm_rows")
        y_copied = sem("y_copied")
        bx_sum = sem("bx_sum")
        bx_exp = sem("bx_exp")
        bv_part = sem("bv_part")
        bv_copy = sem("bv_copy")
        bv_turned = sem("bv_turned")
        bv_rows = sem("bv_rows")
        o_split = sem("o_split")
        o_turned = sem("o_turned")
        o_cols = sem("o_cols")
        o_proj = sem("o_proj")
        o_rows = sem("o_rows")
        norm_sum_y = sem("norm_sum_y")
        norm_root_y = sem("norm_root_y")
        f_split = sem("f_split")
        f_turned = sem("f_turned")
        f_cols = sem("f_cols")
        r_proj = sem("r_proj")
        r_rows = sem("r_rows")
        r_in = sem("r_in")
        r_exp = sem("r_exp")
        w_split = sem("w_split")
        w_turned = sem("w_turned")
        w_cols = sem("w_cols")
        e_sum = sem("e_sum")
        e_silu = sem("e_silu")
        e_mul = sem("e_mul")
        e_weigh = sem("e_weigh")
        e_hid = sem("e_hid")
        e_part = sem("e_part")
        e_copy = sem("e_copy")
        e_turned = sem("e_turned")
        e_rows = sem("e_rows")
        hr_done = sem("hr_done")
        stored = sem("stored")
        step_x = sem("step_x")
        step_y = sem("step_y")
        pool_x = sem("pool_x")
        pool_y = sem("pool_y")
        loop_sems = sem_nums[first_loop_sem:]
        assert max(loop_sems) - min(loop_sems) == len(loop_sems) - 1

        def tile(t):
            return slice(t * P, (t + 1) * P)

        def cols(c):
            return slice(c * CW, (c + 1) * CW)

        def half(c):
            return slice(c * HALF, (c + 1) * HALF)

        def kept(c, jt):
            off = max(0, (jt - 3 * c) * P)
            return off, min(off, CW - 256)

        def flat3(ap):
            return ap.rearrange("p a b -> p (a b)")

        ORDER = [0, 2, 1, 3]
        PER_HEAD = sum(count for count, _ in CHUNKS)
        CAUSAL = [(c, n, jt) for c in range(NC3) for jt in range(3 * c + 3) for n in range(NH)]
        CAUSAL_END = [12, 36, 72]
        DOWN = 2
        MIX = 3
        PAIRS = [(2 * i, min(2, NT - 2 * i)) for i in range(5)]

        def added(n):
            return (NT - 1) * (n // NT) + max(n % NT, 1)

        class Banks:

            def __init__(self, banks):
                self.banks, self.n = banks, 0

            def next(self):
                self.n += 1
                return self.banks[(self.n - 1) % len(self.banks)]

        XB, XO = [0, 1], 2
        XB3 = [0, 1, 2]
        YB, YO = [3, 4, 5, 6], 7

        class Filled:

            def __init__(self, pe):
                self.pe, self.reader = pe, {}

            def fill(self, bank, sem_of_reader, value):
                if bank in self.reader:
                    self.pe.wait_ge(*self.reader[bank])
                self.reader[bank] = (sem_of_reader, value)

        def turned3(pe, bank, src, c):
            for t in range(3):
                m = pe.transpose(PS[:, bank, tile(t)], src(3 * c + t), ident[:, :])
            return m

        def both(pe, o, lhs, rhs):
            pe.matmul(o, lhs[0], rhs[0], start=True, stop=False)
            return pe.matmul(o, lhs[1], rhs[1], start=False, stop=True)

        def hi_lo_of(buf, t):
            return buf[:, t, :, :].rearrange("p a c -> p (a c)")

        def mix_tensor(pe, beside):
            banks = Filled(pe)
            xr = Banks(XB3)
            yield "split"
            yield "split"
            pe.wait_ge(x_split, 2)
            for c in range(2):
                k = xr.next()
                banks.fill(k, x_cols, c + 1)
                for t in range(4):
                    m = pe.transpose(PS[:, k, tile(t)], hi_lo_of(hi_lo, 4 * c + t), ident[:, :])
                m.then_inc(x_turned, 1)
                yield "turn"
            for c in range(2):
                pe.wait_ge(x_cols, c + 1)
                for i, w in enumerate((tk_s, tq_s)):
                    k = xr.next()
                    banks.fill(k, kq_lo, 2 * c + i + 1)
                    both(pe, PS[:, k, :], (w[:, 0, :], w[:, 1, :]), (xb[:, half(c)],) * 2).then_inc(kq_sum, 1)
                    yield "project"
            for i in range(4):
                k = xr.next()
                banks.fill(k, v_out, i + 1)
                for s in (2 * i, 2 * i + 1):
                    m = both(pe, PS[:, k, 256 * (s % 2):256 * (s % 2) + 256], (xb[:, tile(s)],) * 2,
                             (vo_s[:, 0, :], vo_s[:, 1, :]))
                m.then_inc(v_sum, 1)
                yield "project"
            xr = Banks(XB)
            pe.wait_ge(kq_lo, 4)
            for n in range(2 * NTI + MIX):
                if n < 2 * NTI:
                    c, s = n // NTI, n % NTI
                    k = xr.next()
                    banks.fill(k, moved, n + 1)
                    both(pe, PS[:, k, :], (ka[:, tile(s)],) * 2, (qa[:, half(c)], qb[:, half(c)])).then_inc(ts_sum, 1)
                if n >= MIX:
                    m = n - MIX
                    c, s = m // NTI, m % NTI
                    if m == 0:
                        pe.wait_ge(v_out, 4)
                    if s == 1:
                        banks.fill(XO, y_cols, c + 1)
                    if s % 2:
                        pe.wait_ge(gated, m + 1)
                        for i in (s - 1, s):
                            h = i % 2
                            pe.matmul(PS[C * h:C * h + C, XO, :], vt[:, i, :], ring[:, (NTI * c + i) % 5, :],
                                      start=(i == h), stop=(i >= NTI - 2)).then_inc(mixed, 1)
                yield "mix"
            yield "rows"
            k = xr.next()
            banks.fill(k, y_biased, 1)
            for t in range(NTI):
                if t % 4 == 0:
                    pe.wait_ge(y_cols, t // 4 + 1)
                m = pe.matmul(PS[:, k, C * t:C * t + C], yT[:, tile(t)], fold[:, :], start=True, stop=True)
            m.then_inc(y_turned, 1)
            yield "rows"
            for _ in range(9):
                yield "norm"
            xr = Banks(XB3)
            pe.wait_ge(a_split, 2)
            for c in range(NC3):
                k = xr.next()
                banks.fill(k, a_cols, c + 1)
                turned3(pe, k, lambda t: hi_lo_of(hi_lo, t), c).then_inc(a_turned, 1)
                yield "turn"
            for c in range(NC3):
                k = xr.next()
                pe.wait_ge(a_cols, c + 1)
                banks.fill(k, aq_lo, c + 1)
                both(pe, PS[:, k, 0:CW], (a_s[:, 0, :], a_s[:, 1, :]), (ka[:, cols(c)],) * 2).then_inc(aq_sum, 1)
                yield "project"
            pe.wait_ge(aq_hi, NC3)
            pe.wait_ge(aq_lo, NC3)
            pe.wait_ge(a_copy, 1)
            pe.wait_ge(a_ones, 2)
            for u in range(3 * NT):
                t, j = u // 3, u % 3
                k = xr.next()
                banks.fill(k, as_max, u + 1)
                js = slice(JW * j, JW * j + JW + 1)
                both(pe, PS[:, k, 0:JW + 1], (qa[:, tile(t)], qb[:, tile(t)]), (ka[:, js], xb[:, js]))\
                    .then_inc(as_sum, 1)
                yield "maxima"
            for c in range(NC3):
                yield "norm"
                k = xr.next()
                pe.wait_ge(am_split, c + 1)
                banks.fill(k, am_rows, c + 1)
                for t in range(3):
                    m = pe.transpose(PS[0:96, k, tile(t)], mp[:, 3 * c + t, :], ident[:, :])
                m.then_inc(am_turned, 1)
                yield "turn"
            xr = Banks(XB)
            pe.wait_ge(am_rows, NC3)

            def turn_back(c):
                k = xr.next()
                pe.wait_ge(av_copy, c + 1)
                pe.wait_ge(at_added, added(NT * (c + 1) - 1))
                banks.fill(k, av_rows, c + 1)
                for t in range(3):
                    pe.matmul(PS[:, k, 66 * t:66 * t + C], oT[:, tile(3 * c + t)], fold[:, :], start=True, stop=True)
                    m = pe.matmul(PS[:, k, 66 * t + C:66 * t + C + 1], sums[:, c % 2, tile(t)], ones[:, :],
                                  start=True, stop=True)
                m.then_inc(av_turned, 1)

            for n in range(3 * NT + 2):
                if n < 3 * NT:
                    c, jt = n // NT, n % NT
                    k = xr.next()
                    banks.fill(k, at_exp, n + 1)
                    both(pe, PS[:, k, 0:CW], (ka[:, tile(jt)], xb[:, tile(jt)]),
                         (qa[:, cols(c)], qb[:, cols(c)])).then_inc(at_sum, 1)
                if n >= 2:
                    c, jt = (n - 2) // NT, (n - 2) % NT
                    if jt == 1:
                        banks.fill(XO, av_copy, c + 1)
                    if jt % 2 or jt == NT - 1:
                        pe.wait_ge(at_exp, n - 1)
                        for i in ((jt - 1, jt) if jt % 2 else (jt,)):
                            h, key = i % 2, KEYS[i]
                            pe.matmul(PS[C * h:C * h + C, XO, 0:CW], xv[0:key, i, :],
                                      ring[0:key, (NT * c + i) % 4, 0:CW], start=(i == h), stop=(i >= NT - 2))\
                                .then_inc(av_part, 1)
                    if jt == 3 and c >= 1:
                        turn_back(c - 1)
                yield "attend"
            turn_back(2)
            yield "rows"
            yield "rows"
            for _ in range(14):
                yield "norm"
            xr = Banks(XB3)
            pe.wait_ge(b_split, 2)
            for c in range(NC3):
                k = xr.next()
                banks.fill(k, b_cols, c + 1)
                turned3(pe, k, lambda t: hi_lo_of(hi_lo, t), c).then_inc(b_turned, 1)
                yield "turn"
            for i, (t0, m) in enumerate(PAIRS):
                k = xr.next()
                banks.fill(k, b_v, i + 1)
                for t in range(t0, t0 + m):
                    if t % 3 == 0:
                        pe.wait_ge(b_cols, t // 3 + 1)
                    last = both(pe, PS[:, k, 256 * (t % 2):256 * (t % 2) + 256], (ka[:, tile(t)],) * 2,
                                (qkv_s[:, 0, :], qkv_s[:, 1, :]))
                last.then_inc(b_proj, 1)
                yield "project"
            for _ in range(8):
                yield "slots"
            pe.wait_ge(b_slot, 12)
            for u in range(12):
                src = (kp, qp)[u // 6]
                k = xr.next()
                banks.fill(k, bt_cols, u + 1)
                turned3(pe, k, lambda t: flat3(src[:, t, u // 3 % 2, :, :]), u % 3).then_inc(bt_turned, 1)
                yield "turn"
        def mix_scalar(act, beside):
            xr = Banks(XB3)
            act.wait_ge(x_in, 32)
            act.activation(r(hi_lo[:, 0:NTI, 0, :]), xin, ACT.Copy).then_inc(x_split, 1)
            yield "split"
            yield "split"
            for c in range(2):
                k = xr.next()
                act.wait_ge(x_turned, c + 1)
                act.activation(xb[:, half(c)], PS[:, k, :], ACT.Copy).then_inc(x_cols, 1)
                yield "turn"
            for c in range(2):
                for i, (dst, bias) in enumerate(((ka, bk_c), (qa, bq_c))):
                    k = xr.next()
                    act.wait_ge(kq_sum, 2 * c + i + 1)
                    act.activation(dst[:, half(c)], PS[:, k, :], ACT.Identity, bias=bias[:, 0:1]).then_inc(kq_hi, 1)
                    yield "project"
            for i in range(4):
                xr.next()
                yield "project"
            xr = Banks(XB)
            for n in range(2 * NTI + MIX):
                if n < 2 * NTI:
                    k = xr.next()
                    act.wait_ge(ts_sum, n + 1)
                    if n >= 5:
                        act.wait_ge(mixed, n - 4)
                    act.activation(ring[:, n % 5, :], PS[:, k, :], ACT.Copy).then_inc(moved, 1)
                if n in (NTI + MIX - 1, 2 * NTI + MIX - 1):
                    c = n // NTI - 1
                    act.wait_ge(mixed, NTI * (c + 1))
                    act.activation(yT[:, half(c)], PS[:, XO, :], ACT.Copy).then_inc(y_cols, 1)
                yield "mix"
            yield "rows"
            xr.next()
            yield "rows"
            for _ in range(9):
                yield "norm"
            xr = Banks(XB3)
            for c in range(NC3):
                k = xr.next()
                act.wait_ge(a_turned, c + 1)
                act.activation(ka[:, cols(c)], PS[:, k, 0:CW], ACT.Copy).then_inc(a_cols, 1)
                yield "turn"
            for c in range(NC3):
                k = xr.next()
                act.wait_ge(aq_sum, c + 1)
                act.activation(qa[:, cols(c)], PS[:, k, 0:CW], ACT.Copy).then_inc(aq_hi, 1)
                yield "project"
            for u in range(3 * NT):
                xr.next()
                yield "maxima"
            for c in range(NC3):
                yield "norm"
                k = xr.next()
                act.wait_ge(am_turned, c + 1)
                act.activation(qb[64:66, cols(c)], PS[64:66, k, 0:CW], ACT.Copy).then_inc(am_rows, 1)
                yield "turn"
            xr = Banks(XB)
            for n in range(3 * NT + 2):
                if n < 3 * NT:
                    k = xr.next()
                    act.wait_ge(at_sum, n + 1)
                    if n >= 4:
                        act.wait_ge(av_part, n - 3)
                        act.wait_ge(at_added, added(n - 4))
                    key = KEYS[n % NT]
                    act.activation(ring[0:key, n % 4, 0:CW], PS[0:key, k, 0:CW], ACT.Exp, scale=C ** -0.5)\
                        .then_inc(at_exp, 1)
                if n >= NT + 1 and (n - 1) % NT == 0:
                    c = (n - 1) // NT - 1
                    act.wait_ge(av_part, NT * (c + 1))
                    act.activation(oT[:, cols(c)], PS[:, XO, 0:CW], ACT.Copy).then_inc(av_copy, 1)
                if n >= 2 and (n - 2) % NT == 3 and n - 2 > NT:
                    xr.next()
                yield "attend"
            xr.next()
            yield "rows"
            yield "rows"
            for _ in range(14):
                yield "norm"
            xr = Banks(XB3)
            for c in range(NC3):
                k = xr.next()
                act.wait_ge(b_turned, c + 1)
                act.activation(ka[:, cols(c)], PS[:, k, 0:CW], ACT.Copy).then_inc(b_cols, 1)
                yield "turn"
            if beside:
                act.wait_ge(bv_part, len(CAUSAL))
            for i, (t0, m) in enumerate(PAIRS):
                k = xr.next()
                act.wait_ge(b_rope, 2 * (i + 1))
                act.activation(vv[:, t0:t0 + m, :, 0:HD],
                               PS[:, k, 0:256 * m].rearrange("p (t n) -> p t n", t=m)[:, :, 96:128]
                               .rearrange("p t (k d) -> p t k d", k=NKV), ACT.Copy).then_inc(b_v, 1)
                yield "project"
            for _ in range(8):
                yield "slots"
            for u in range(12):
                k = xr.next()
                act.wait_ge(bt_turned, u + 1)
                act.activation((kT, qT)[u // 6][:, u // 3 % 2, cols(u % 3)], PS[:, k, 0:CW], ACT.Copy).then_inc(bt_cols, 1)
                yield "turn"
        def mix_vector(dve, beside):
            xr = Banks(XB3)
            taken = [0]

            def step(ins):
                taken[0] += 1
                ins.then_inc(step_x, 1)

            def done():
                dve.wait_ge(step_x, taken[0])

            def split(src, n, counted):
                dve.tensor_copy(r(hi_lo[:, 0:n, 0, :]), src).then_inc(counted, 1)
                yield
                dve.wait_ge(counted, 1)
                dve.tensor_tensor(r(hi_lo[:, 0:n, 1, :]), src, hi_lo[:, 0:n, 0, :], ALU.subtract).then_inc(counted, 1)
                yield

            def centre(src):
                step(dve.tensor_reduce(st[:, 0, :], src, AX.X, ALU.add))
                yield
                done()
                step(dve.tensor_scalar(st[:, 4, :], st[:, 0, :], -1.0 / C, None, ALU.mult))
                yield
                done()
                step(dve.tensor_tensor(xc[:, :, :], src, spread(st[:, 4, :], C), ALU.add))
                yield

            def squares(src):
                done()
                step(dve.tensor_tensor(sq[:, :, :], src, src, ALU.mult))
                yield
                done()
                dve.tensor_reduce(st[:, 1, :], sq[:, :, :], AX.X, ALU.add).then_inc(norm_sum, 1)
                yield

            yield "split"
            dve.wait_ge(x_split, 1)
            dve.tensor_tensor(r(hi_lo[:, 0:NTI, 1, :]), xin, hi_lo[:, 0:NTI, 0, :], ALU.subtract).then_inc(x_split, 1)
            yield "split"
            for c in range(2):
                xr.next()
                yield "turn"
            for c in range(2):
                k = xr.next()
                dve.wait_ge(kq_hi, 2 * c + 1)
                dve.scalar_tensor_tensor(ka[64:128, half(c)], PS[64:128, k, :], bk_c[64:128, 0:1],
                                         f(ka[64:128, half(c)]), ALU.add, ALU.subtract).then_inc(kq_lo, 1)
                yield "project"
                k = xr.next()
                dve.wait_ge(kq_hi, 2 * c + 2)
                dve.scalar_tensor_tensor(qb[:, half(c)], PS[:, k, :], bq_c[:, 0:1], f(qa[:, half(c)]),
                                         ALU.add, ALU.subtract).then_inc(kq_lo, 1)
                yield "project"
            for i in range(4):
                k = xr.next()
                dve.wait_ge(v_sum, i + 1)
                dve.tensor_tensor(vt[:, 2 * i:2 * i + 2, :], PS[:, k, :].rearrange("p (t n) -> p t n", t=2)[:, :, 0:C],
                                  every(bv_row[:, :], 2), ALU.add).then_inc(v_out, 1)
                yield "project"
            xr = Banks(XB)
            for n in range(2 * NTI + MIX):
                if n < 2 * NTI:
                    xr.next()
                yield "mix"
            yield "rows"
            k = xr.next()
            dve.wait_ge(y_turned, 1)
            dve.tensor_tensor(xin, PS[:, k, :].rearrange("p (t c) -> p t c", t=NTI), every(bo_row[:, :], NTI), ALU.add)\
                .then_inc(y_biased, 1)
            dve.wait_ge(y_biased, 1)
            step(dve.tensor_scalar(vt, xin, 0.0, a_c[:, 0:1], ALU.min, ALU.mult))
            done()
            dve.scalar_tensor_tensor(H[:, 0:NTI, :], xin, 0.0, vt, ALU.max, ALU.add).then_inc(h_rows, 1)
            yield "rows"
            dve.wait_ge(h_rows, 1)
            for _ in centre(H[:, :, :]):
                yield "norm"
            for _ in squares(xc[:, :, :]):
                yield "norm"
            yield "norm"
            dve.wait_ge(norm_root, 1)
            step(dve.tensor_tensor(xv[:, :, 0:C], xc[:, :, :], spread(st[:, 3, :], C), ALU.mult))
            yield "norm"
            done()
            for _ in split(xv[:, :, 0:C], NT, a_split):
                yield "norm"
            xr = Banks(XB3)
            for c in range(NC3):
                xr.next()
                yield "turn"
            for c in range(NC3):
                k = xr.next()
                if c == 0:
                    dve.wait_ge(a_cols, NC3)
                    dve.tensor_copy(xb[0:C, :], f(ka[0:C, :])).then_inc(a_copy, 1)
                dve.wait_ge(aq_hi, c + 1)
                dve.tensor_tensor(qb[0:C, cols(c)], PS[0:C, k, 0:CW], f(qa[0:C, cols(c)]), ALU.subtract).then_inc(aq_lo, 1)
                yield "project"
            for u in range(3 * NT):
                t, j = u // 3, u % 3
                k = xr.next()
                dve.wait_ge(as_sum, u + 1)
                dve.tensor_reduce(nmp[:, t, j:j + 1], PS[:, k, 0:JW], AX.X, ALU.max, negate=True).then_inc(as_max, 1)
                yield "maxima"
            for c in range(NC3):
                ts = slice(3 * c, 3 * c + 3)
                dve.wait_ge(as_max, 9 * (c + 1))
                step(dve.tensor_reduce(nm[:, ts], nmp[:, ts, :], AX.X, ALU.min))
                done()
                m3 = nm[:, ts].unsqueeze(2)
                step(dve.tensor_copy(r(mp[:, ts, 64:65]), m3))
                done()
                dve.tensor_tensor(r(mp[:, ts, 65:66]), m3, mp[:, ts, 64:65], ALU.subtract).then_inc(am_split, 1)
                yield "norm"
                xr.next()
                yield "turn"
            xr = Banks(XB)

            def attended(c):
                cs = slice(3 * c, 3 * c + 3)
                k = xr.next()
                dve.wait_ge(av_turned, c + 1)
                o = PS[:, k, 0:3 * 66].rearrange("p (t n) -> p t n", t=3)
                step(dve.reciprocal(rden[:, cs, :], o[:, :, 64:65]))
                done()
                dve.tensor_tensor(sq[:, cs, :], o[:, :, 0:C], rden[:, cs, :].broadcast_to([P, 3, C]), ALU.mult)\
                    .then_inc(av_rows, 1)
                dve.wait_ge(av_rows, c + 1)
                if beside and c == 0:
                    dve.wait_ge(y_copied, 2)
                step(dve.tensor_tensor(H2[:, cs, :], H[:, cs, :], sq[:, cs, :], ALU.add))

            for n in range(3 * NT + 2):
                if n < 3 * NT:
                    xr.next()
                if n >= 2 and (n - 2) % NT == 3 and n - 2 > NT:
                    attended((n - 2) // NT - 1)
                yield "attend"
            attended(2)
            yield "rows"
            done()
            yield "rows"
            for _ in centre(H2[:, :, :]):
                yield "norm"
            for _ in squares(xc[:, :, :]):
                yield "norm"
            yield "norm"
            dve.wait_ge(norm_root, 2)
            step(dve.tensor_tensor(Y[:, :, :], xc[:, :, :], spread(st[:, 3, :], C), ALU.mult))
            yield "norm"
            for _ in squares(Y[:, :, :]):
                yield "norm"
            step(dve.tensor_tensor(xc[:, :, :], Y[:, :, :], every(ln1_b[:, :], NT), ALU.mult))
            yield "norm"
            yield "norm"
            dve.wait_ge(norm_root, 3)
            done()
            step(dve.tensor_tensor(hn, xc[:, :, :], spread(st[:, 3, :], C), ALU.mult))
            yield "norm"
            done()
            for _ in split(hn, NT, b_split):
                yield "norm"
            xr = Banks(XB3)
            for c in range(NC3):
                xr.next()
                yield "turn"
            for i, (t0, m) in enumerate(PAIRS):
                k = xr.next()
                ts = slice(t0, t0 + m)
                dve.wait_ge(b_proj, i + 1)
                o = PS[:, k, 0:256 * m].rearrange("p (t n) -> p t n", t=m)
                for part, table in ((0, cos), (1, sin)):
                    dve.tensor_tensor(rot[:, part, ts, :].rearrange("p t (h d) -> p t h d", h=6),
                                      o[:, :, P * part:P * part + 96].rearrange("p t (h d) -> p t h d", h=6),
                                      table[:, ts, :].unsqueeze(2).broadcast_to([P, m, 6, HD]), ALU.mult)\
                        .then_inc(b_rope, 1)
                yield "project"
            dve.wait_ge(b_rope, 10)
            step(dve.tensor_tensor(qk, rot[:, 0, :, :], rot[:, 1, :, :], ALU.add))
            yield "slots"
            done()
            for slot in (0, 1, 2):
                for p in range(2):
                    src = qk[:, :, 0:C].rearrange("p t (a b d) -> p t a b d", a=2, b=2)[:, :, :, p, :]
                    dst = [qp[:, :, p, s, :].rearrange("p t (a d) -> p t a d", a=2) for s in range(3)]
                    if slot < 2:
                        dve.tensor_copy(r(dst[slot]), src).then_inc(b_slot, 1)
                    else:
                        dve.wait_ge(b_slot, 4)
                        dve.tensor_tensor(r(dst[2]), src, dst[0], ALU.subtract).then_inc(b_slot, 1)
                yield "slots"
            for slot in (0, 2, 1):
                for g in range(NKV):
                    src = qk[:, :, C + HD * g:C + HD * g + HD]
                    dst = [kp[:, :, g, s, HD * g:HD * g + HD] for s in range(3)]
                    if slot != 1:
                        dve.tensor_copy(r(dst[slot]), src).then_inc(b_slot, 1)
                    else:
                        dve.wait_ge(b_slot, 10)
                        dve.tensor_tensor(r(dst[1]), src, dst[0], ALU.subtract).then_inc(b_slot, 1)
                yield "slots"
            yield "slots"
            for u in range(12):
                xr.next()
                yield "turn"

        def root(pool, st, eps, summed, n, stepped, rooted):
            pool.wait_ge(summed, n + 1)
            pool.tensor_scalar(st[:, 2, :], st[:, 1, :], 1.0 / C, eps, ALU.mult, ALU.add).then_inc(stepped, 1)
            pool.wait_ge(stepped, n + 1)
            pool.tensor_tensor(st[:, 3, :], st[:, 2, :], nhalf[:, 0:1].broadcast_to([P, NT]), ALU.pow).then_inc(rooted, 1)
            pool.wait_ge(rooted, n + 1)

        def mix_pool(pool, names):
            norms = attends = mixes = 0
            for name in names:
                if name == "mix":
                    n, mixes = mixes, mixes + 1
                    if n < 2 * NTI:
                        pool.wait_ge(moved, n + 1)
                        pool.tensor_tensor(ring[:, n % 5, :], ring[:, n % 5, :], gT[:, n % NTI, half(n // NTI)], ALU.mult)\
                            .then_inc(gated, 1)
                if name == "attend":
                    n, attends = attends, attends + 1
                    c, jt = n // NT, n % NT
                    if n < 3 * NT and jt:
                        key = KEYS[jt]
                        pool.wait_ge(at_exp, n + 1)
                        if jt > 1 or c:
                            pool.wait_ge(at_added, added(n) - 1)
                        if jt == 1 and c == 2:
                            pool.wait_ge(av_turned, c - 1)
                        total = sums[0:key, c % 2, :]
                        pool.tensor_tensor(total, ring[0:key, (n - 1) % 4, 0:CW] if jt == 1 else total,
                                           ring[0:key, n % 4, 0:CW], ALU.add).then_inc(at_added, 1)
                        if jt == NT - 1:
                            pool.wait_ge(at_added, added(n))
                elif name == "norm":
                    norms += 1
                    if norms == 5 + 1:
                        root(pool, st, LN_EPS, norm_sum, 0, pool_x, norm_root)
                        pool.wait_ge(mixed, 2 * NTI)
                        pool.memset(f(xb[64:66, :]), 1.0).then_inc(a_ones, 1)
                        pool.wait_ge(a_ones, 1)
                        pool.memset(f(qb[64:128, :]), 0.0).then_inc(a_ones, 1)
                        pool.wait_ge(a_ones, 2)
                    elif norms == 9 + 3 + 5 + 1:
                        root(pool, st, LN_EPS, norm_sum, 1, pool_x, norm_root)
                    elif norms == 9 + 3 + 10:
                        root(pool, st, RMS_EPS, norm_sum, 2, pool_x, norm_root)
                yield name

        def out_tensor(pe):
            banks = Filled(pe)
            yr = Banks(YB)
            yield "copy"
            for i, n in enumerate(ORDER):
                for t in range(NT):
                    count, wide = CHUNKS[t]
                    for j in range(count):
                        k = yr.next()
                        banks.fill(k, bs_max, PER_HEAD * i + sum(m for m, _ in CHUNKS[:t]) + j + 1)
                        last = j == count - 1
                        m = pe.matmul(PS[:, k, 0:wide], qT[:, n % 2, tile(t)], kT[:, n // 2, wide * j:wide * j + wide],
                                      start=True, stop=not last)
                        if last:
                            at = t * P - wide * (count - 1)
                            diag = P if t < NT - 1 else 3 * 368 - NTI * P
                            m = pe.matmul(PS[:, k, at:at + diag], identb[:, :], maskb[:, 0, 0:diag], start=False, stop=True)
                        m.then_inc(bs_sum, 1)
                        yield "maxima"
                yield "norm"
                if i >= 2:
                    p = i - 2
                    for c in range(NC3):
                        k = yr.next()
                        pe.wait_ge(bm_split, 2 * (p + 1))
                        banks.fill(k, bm_rows, 3 * p + c + 1)
                        for t in range(3):
                            m = pe.matmul(PS[96:128, k, tile(t)], mp4[:, 3 * c + t, p, :], ident[:, :], start=True, stop=True)
                        m.then_inc(bm_turned, 1)
                        yield "turn"
            pe.wait_ge(bm_rows, 2 * NC3)

            def turn_back(c):
                k = yr.next()
                pe.wait_ge(bv_copy, c + 1)
                banks.fill(k, bv_rows, c + 1)
                turned3(pe, k, lambda t: oT_y[:, tile(t)], c).then_inc(bv_turned, 1)

            for u in range(len(CAUSAL) + 2):
                if u < len(CAUSAL):
                    c, n, jt = CAUSAL[u]
                    k = yr.next()
                    banks.fill(k, bx_exp, u + 1)
                    keep, o = kept(c, jt)
                    masked = jt >= 3 * c
                    m = pe.matmul(PS[:, k, o:CW], kT[:, n // 2, tile(jt)], qT[:, n % 2, c * CW + o:(c + 1) * CW],
                                  start=True, stop=not masked)
                    if masked:
                        m = pe.matmul(PS[:, k, keep:keep + P], identb[:, :], maskb[:, 1, :], start=False, stop=True)
                    m.then_inc(bx_sum, 1)
                if u >= 2:
                    v = u - 2
                    c, last, jt = CAUSAL[v]
                    if last == NH - 1:
                        if jt == 0:
                            banks.fill(YO, bv_copy, c + 1)
                        pe.wait_ge(bx_exp, v + 1)
                        keep, _ = kept(c, jt)
                        key = KEYS[jt]
                        for n in range(NH):
                            pe.matmul(PS[32 * n:32 * n + 32, YO, keep:CW], vv[0:key, jt, n // 2, :],
                                      ring_y[0:key, (v - NH + 1 + n) % 8, keep:CW], start=(jt == 0),
                                      stop=(jt == 3 * c + 2)).then_inc(bv_part, 1)
                    if v - 3 in CAUSAL_END:
                        turn_back(c - 1)
                yield "causal"
            turn_back(2)
            yield "back"
            yield "norm"
            yield "norm"
            pe.wait_ge(o_split, 2)
            for c in range(NC3):
                k = yr.next()
                banks.fill(k, o_cols, c + 1)
                turned3(pe, k, lambda t: f(hi_lo_of(hi_lo_y, t)), c).then_inc(o_turned, 1)
                yield "turn"

            def rows(w, turned, counted, reader):
                for i, (t0, m) in enumerate(PAIRS):
                    k = yr.next()
                    banks.fill(k, reader, i + 1)
                    for t in range(t0, t0 + m):
                        if t % 3 == 0:
                            pe.wait_ge(turned, t // 3 + 1)
                        last = both(pe, PS[:, k, 256 * (t % 2):256 * (t % 2) + 256], (fT[:, tile(t)],) * 2,
                                    (w[:, 0, :], w[:, 1, :]))
                    last.then_inc(counted, 1)
                    yield "project"

            yield from rows(wo_s, o_cols, o_proj, o_rows)
            for _ in range(8):
                yield "norm"
            pe.wait_ge(f_split, 2)
            for c in range(NC3):
                k = yr.next()
                banks.fill(k, f_cols, c + 1)
                turned3(pe, k, lambda t: f(hi_lo_of(hi_lo_y, t)), c).then_inc(f_turned, 1)
                yield "turn"
            yield from rows(rw_s, f_cols, r_proj, r_rows)
            for _ in range(16):
                yield "route"
            pe.wait_ge(w_split, 2)
            for c in range(NC3):
                k = yr.next()
                banks.fill(k, w_cols, c + 1)
                for t in range(3):
                    m = pe.transpose(PS[0:16, k, tile(t)], wp[:, 3 * c + t, :], ident[:, :])
                m.then_inc(w_turned, 1)
                yield "turn"
            pe.wait_ge(w_cols, NC3)
            for u in range(NC3 * NG + DOWN):
                if u < NC3 * NG:
                    c, g = u // NG, u % NG
                    gs = slice(g * P, g * P + GW[g])
                    fc = (fT[:, cols(c)],) * 2
                    k = yr.next()
                    banks.fill(k, e_silu, u + 1)
                    both(pe, PS[0:GW[g], k, 0:CW], (w1_s[:, 0, gs], w1_s[:, 1, gs]), fc).then_inc(e_sum, 1)
                    k = yr.next()
                    banks.fill(k, e_mul, u + 1)
                    both(pe, PS[0:GW[g], k, 0:CW], (w3_s[:, 0, gs], w3_s[:, 1, gs]), fc).then_inc(e_sum, 1)
                    k = yr.next()
                    banks.fill(k, e_weigh, u + 1)
                    pe.matmul(PS[0:GW[g], k, 0:CW], sel[:, gs], wT[:, cols(c)], start=True, stop=True).then_inc(e_sum, 1)
                if u >= DOWN:
                    v = u - DOWN
                    c, g = v // NG, v % NG
                    if g == 1:
                        banks.fill(YO, e_copy, c + 1)
                    if g % 2 or g == NG - 1:
                        pe.wait_ge(e_hid, v + 1)
                        for i in ((g - 1, g) if g % 2 else (g,)):
                            h = i % 2
                            pe.matmul(PS[C * h:C * h + C, YO, 0:CW], w2_s[0:GW[i], i, :],
                                      hid[0:GW[i], (NG * c + i) % 4, :], start=(i == h), stop=(i >= NG - 2))\
                                .then_inc(e_part, 1)
                yield "expert"
                if u > NG + DOWN and (u - DOWN) % NG == 1:
                    yield from back(pe, banks, yr, (u - DOWN) // NG - 1)
            yield "back"
            yield from back(pe, banks, yr, 2)

        def back(pe, banks, yr, c):
            k = yr.next()
            pe.wait_ge(e_copy, c + 1)
            banks.fill(k, e_rows, c + 1)
            for t in range(3):
                m = pe.matmul(PS[:, k, C * t:C * t + C], oT_y[:, tile(3 * c + t)], fold[:, :], start=True, stop=True)
            m.then_inc(e_turned, 1)
            yield "back"

        def out_scalar(act):
            yr = Banks(YB)
            yield "copy"
            for i in range(NH):
                for _ in range(PER_HEAD):
                    yr.next()
                    yield "maxima"
                yield "norm"
                if i >= 2:
                    for c in range(NC3):
                        k = yr.next()
                        act.wait_ge(bm_turned, 3 * (i - 2) + c + 1)
                        act.activation(qT[96:100, i - 2, cols(c)], PS[96:100, k, 0:CW], ACT.Copy).then_inc(bm_rows, 1)
                        yield "turn"
            for u in range(len(CAUSAL) + 2):
                if u < len(CAUSAL):
                    c, n, jt = CAUSAL[u]
                    k = yr.next()
                    act.wait_ge(bx_sum, u + 1)
                    if u >= 8:
                        act.wait_ge(bv_part, u - 7)
                    key = KEYS[jt]
                    keep, _ = kept(c, jt)
                    act.activation(ring_y[0:key, u % 8, keep:CW], PS[0:key, k, keep:CW], ACT.Exp, scale=HD ** -0.5)\
                        .then_inc(bx_exp, 1)
                if u - 1 in CAUSAL_END:
                    c = CAUSAL_END.index(u - 1)
                    act.wait_ge(bv_part, CAUSAL_END[c])
                    act.activation(oT_y[:, cols(c)], PS[:, YO, 0:CW], ACT.Copy).then_inc(bv_copy, 1)
                if u - 5 in CAUSAL_END:
                    yr.next()
                yield "causal"
            yr.next()
            yield "back"
            yield "norm"
            yield "norm"

            def columns(turned, counted):
                for c in range(NC3):
                    k = yr.next()
                    act.wait_ge(turned, c + 1)
                    act.activation(fT[:, cols(c)], PS[:, k, 0:CW], ACT.Copy).then_inc(counted, 1)
                    yield "turn"

            yield from columns(o_turned, o_cols)
            for _ in PAIRS:
                yr.next()
                yield "project"
            for _ in range(8):
                yield "norm"
            yield from columns(f_turned, f_cols)
            for _ in PAIRS:
                yr.next()
                yield "project"
            for i in range(16):
                if i == 2:
                    act.wait_ge(r_in, 1)
                    act.activation(pr[:, :, :], lg[:, :, :], ACT.Exp).then_inc(r_exp, 1)
                yield "route"
            for c in range(NC3):
                k = yr.next()
                act.wait_ge(w_turned, c + 1)
                act.activation(wT[0:16, cols(c)], PS[0:16, k, 0:CW], ACT.Copy).then_inc(w_cols, 1)
                yield "turn"
            for u in range(NC3 * NG + DOWN):
                if u < NC3 * NG:
                    g = u % NG
                    k = yr.next()
                    yr.next()
                    act.wait_ge(e_sum, 3 * u + 1)
                    if u >= 2:
                        act.wait_ge(e_mul, u - 1)
                    act.activation(ring_y[0:GW[g], u % 2, :], PS[0:GW[g], k, 0:CW], ACT.Silu).then_inc(e_silu, 1)
                    k = yr.next()
                    act.wait_ge(e_sum, 3 * u + 3)
                    if u >= 4:
                        act.wait_ge(e_part, u - 3)
                    act.activation(hid[0:GW[g], u % 4, :], PS[0:GW[g], k, 0:CW], ACT.Copy).then_inc(e_weigh, 1)
                if u >= DOWN and (u - DOWN) % NG == NG - 1:
                    c = (u - DOWN) // NG
                    act.wait_ge(e_part, NG * (c + 1))
                    act.activation(oT_y[:, cols(c)], PS[:, YO, 0:CW], ACT.Copy).then_inc(e_copy, 1)
                yield "expert"
                if u > NG + DOWN and (u - DOWN) % NG == 1:
                    yr.next()
                    yield "back"
            yield "back"
            yr.next()
            yield "back"

        def out_vector(dve):
            yr = Banks(YB)
            taken = [0]

            def step(ins):
                taken[0] += 1
                ins.then_inc(step_y, 1)

            def done():
                dve.wait_ge(step_y, taken[0])

            def split(src, counted):
                dve.tensor_copy(hi_lo_y[:, :, 0, :], src).then_inc(counted, 1)
                yield
                dve.wait_ge(counted, 1)
                dve.tensor_tensor(hi_lo_y[:, :, 1, :], src, f(hi_lo_y[:, :, 0, :]), ALU.subtract).then_inc(counted, 1)
                yield

            dve.tensor_copy(H2y[:, :, :], H2[:, :, :]).then_inc(y_copied, 1)
            dve.tensor_copy(R1[:, :, :], Y[:, :, :]).then_inc(y_copied, 1)
            yield "copy"

            for i, n in enumerate(ORDER):
                for t in range(NT):
                    count, wide = CHUNKS[t]
                    for j in range(count):
                        k = yr.next()
                        u = PER_HEAD * i + sum(m for m, _ in CHUNKS[:t]) + j
                        dve.wait_ge(bs_sum, u + 1)
                        dst = nm4[:, n, t:t + 1] if count == 1 else nmp_y[:, t, j:j + 1]
                        dve.tensor_reduce(dst, PS[:, k, 0:(wide if t else P)], AX.X, ALU.max, negate=True)\
                            .then_inc(bs_max, 1)
                        yield "maxima"
                dve.wait_ge(bs_max, PER_HEAD * (i + 1))
                step(dve.tensor_reduce(nm4[:, n, 4:8], nmp_y[:, 4:8, 0:2], AX.X, ALU.min))
                step(dve.tensor_reduce(nm4[:, n, 8:9], nmp_y[:, 8, :], AX.X, ALU.min))
                done()
                m4, at = nm4[:, n, :].unsqueeze(2), 2 * (n // 2)
                step(dve.tensor_copy(r(mp4[:, :, n % 2, at:at + 1]), m4))
                done()
                dve.tensor_tensor(r(mp4[:, :, n % 2, at + 1:at + 2]), m4, mp4[:, :, n % 2, at:at + 1],
                                  ALU.subtract).then_inc(bm_split, 1)
                yield "norm"
                if i >= 2:
                    for c in range(NC3):
                        yr.next()
                        yield "turn"

            def attended(c):
                cs = slice(3 * c, 3 * c + 3)
                k = yr.next()
                dve.wait_ge(bv_turned, c + 1)
                o = PS[:, k, 0:CW].rearrange("p (t h d) -> p t h d", t=3, h=NH)
                step(dve.reciprocal(rden_y[:, cs, :].unsqueeze(3), o[:, :, :, 16:17]))
                done()
                dve.tensor_tensor(hn_y[:, cs, :].rearrange("p t (h d) -> p t h d", h=NH), o[:, :, :, 0:HD],
                                  rden_y[:, cs, :].unsqueeze(3).broadcast_to([P, 3, NH, HD]), ALU.mult)\
                    .then_inc(bv_rows, 1)

            for u in range(len(CAUSAL) + 2):
                if u < len(CAUSAL):
                    yr.next()
                if u - 5 in CAUSAL_END:
                    attended(CAUSAL_END.index(u - 5))
                yield "causal"
            attended(2)
            yield "back"
            dve.wait_ge(bv_rows, NC3)
            for _ in split(hn_y[:, :, :], o_split):
                yield "norm"
            for c in range(NC3):
                yr.next()
                yield "turn"
            for i, (t0, m) in enumerate(PAIRS):
                k = yr.next()
                ts = slice(t0, t0 + m)
                if i == 0:
                    dve.wait_ge(y_copied, 2)
                dve.wait_ge(o_proj, i + 1)
                o = PS[:, k, 0:256 * m].rearrange("p (t n) -> p t n", t=m)
                dve.tensor_tensor(R1[:, ts, :], o[:, :, 0:C], R1[:, ts, :], ALU.add).then_inc(o_rows, 1)
                yield "project"
            dve.wait_ge(o_rows, 5)
            step(dve.tensor_tensor(sq_y, R1[:, :, :], R1[:, :, :], ALU.mult))
            yield "norm"
            done()
            dve.tensor_reduce(sty[:, 1, :], sq_y, AX.X, ALU.add).then_inc(norm_sum_y, 1)
            yield "norm"
            step(dve.tensor_tensor(xc_y, R1[:, :, :], every(ln2_b[:, :], NT), ALU.mult))
            yield "norm"
            yield "norm"
            dve.wait_ge(norm_root_y, 1)
            done()
            step(dve.tensor_tensor(hn_y[:, :, :], xc_y, spread(sty[:, 3, :], C), ALU.mult))
            yield "norm"
            done()
            for _ in split(hn_y[:, :, :], f_split):
                yield "norm"
            yield "norm"
            for c in range(NC3):
                yr.next()
                yield "turn"
            for i, (t0, m) in enumerate(PAIRS):
                k = yr.next()
                dve.wait_ge(r_proj, i + 1)
                o = PS[:, k, 0:256 * m].rearrange("p (t n) -> p t n", t=m)
                dve.tensor_copy(lg[:, t0:t0 + m, :], o[:, :, 0:NE]).then_inc(r_rows, 1)
                yield "project"
            dve.wait_ge(r_rows, 5)
            step(dve.tensor_reduce(sty[:, 5, :], lg[:, :, :], AX.X, ALU.max))
            yield "route"
            done()
            dve.tensor_tensor(lg[:, :, :], lg[:, :, :], spread(sty[:, 5, :], NE), ALU.subtract).then_inc(r_in, 1)
            yield "route"
            yield "route"
            dve.wait_ge(r_exp, 1)
            step(dve.tensor_reduce(sty[:, 6, :], pr[:, :, :], AX.X, ALU.add))
            yield "route"
            done()
            step(dve.reciprocal(sty[:, 7, :], sty[:, 6, :]))
            yield "route"
            done()
            step(dve.tensor_tensor(pr[:, :, :], pr[:, :, :], spread(sty[:, 7, :], NE), ALU.mult))
            yield "route"
            done()
            mine = pr[:, :, :].unsqueeze(3).broadcast_to([P, NT, NE, NE])
            other = pr[:, :, :].unsqueeze(2).broadcast_to([P, NT, NE, NE])
            c4 = [cmp[:, i, :, :].rearrange("p t (a b) -> p t a b", a=NE) for i in range(2)]
            dve.tensor_tensor(c4[0], other, mine, ALU.is_gt)
            yield "route"
            step(dve.tensor_tensor(c4[1], other, mine, ALU.is_equal))
            yield "route"
            done()
            step(dve.tensor_tensor(cmp[:, 1, :, :], cmp[:, 1, :, :], every(tri[:, :], NT), ALU.mult))
            yield "route"
            done()
            step(dve.tensor_tensor(cmp[:, 0, :, :], cmp[:, 0, :, :], cmp[:, 1, :, :], ALU.add))
            yield "route"
            done()
            step(dve.tensor_reduce(wt[:, :, :], c4[0], AX.X, ALU.add))
            yield "route"
            done()
            step(dve.scalar_tensor_tensor(wt[:, :, :], wt[:, :, :], 1.5, pr[:, :, :], ALU.is_lt, ALU.mult))
            yield "route"
            done()
            step(dve.tensor_reduce(sty[:, 5, :], wt[:, :, :], AX.X, ALU.add))
            yield "route"
            done()
            step(dve.tensor_scalar(sty[:, 6, :], sty[:, 5, :], 1e-9, None, ALU.add))
            done()
            step(dve.reciprocal(sty[:, 7, :], sty[:, 6, :]))
            yield "route"
            done()
            step(dve.tensor_tensor(wt[:, :, :], wt[:, :, :], spread(sty[:, 7, :], NE), ALU.mult))
            yield "route"
            done()
            dve.tensor_copy(r(wp[:, :, 0:NE]), wt[:, :, :]).then_inc(w_split, 1)
            dve.wait_ge(w_split, 1)
            dve.tensor_tensor(r(wp[:, :, NE:16]), wt[:, :, :], wp[:, :, 0:NE], ALU.subtract).then_inc(w_split, 1)
            yield "route"
            for c in range(NC3):
                yr.next()
                yield "turn"

            def e_result(c):
                cs = slice(3 * c, 3 * c + 3)
                k = yr.next()
                dve.wait_ge(e_turned, c + 1)
                dve.tensor_tensor(R1[:, cs, :], PS[:, k, 0:3 * C].rearrange("p (t n) -> p t n", t=3),
                                  H2y[:, cs, :], ALU.add).then_inc(e_rows, 1)

            dve.wait_ge(hr_done, 1)
            for u in range(NC3 * NG + DOWN):
                if u < NC3 * NG:
                    gw = GW[u % NG]
                    yr.next()
                    k = yr.next()
                    yr.next()
                    dve.wait_ge(e_sum, 3 * u + 2)
                    dve.wait_ge(e_silu, u + 1)
                    if u >= 2:
                        dve.wait_ge(e_hid, u - 1)
                    dve.tensor_tensor(ring_y[0:gw, 2 + u % 2, :], PS[0:gw, k, 0:CW], ring_y[0:gw, u % 2, :], ALU.mult)\
                        .then_inc(e_mul, 1)
                yield "expert"
                if u > NG + DOWN and (u - DOWN) % NG == 1:
                    e_result((u - DOWN) // NG - 1)
                    yield "back"
            yield "back"
            e_result(2)
            yield "back"

        def out_pool(pool, names):
            norms = experts = 0
            for name in names:
                if name == "expert":
                    u, experts = experts, experts + 1
                    if u < NC3 * NG:
                        pool.wait_ge(e_mul, u + 1)
                        pool.wait_ge(e_weigh, u + 1)
                        pool.tensor_tensor(hid[:, u % 4, :], ring_y[:, 2 + u % 2, :], hid[:, u % 4, :], ALU.mult)\
                            .then_inc(e_hid, 1)
                elif name == "norm":
                    norms += 1
                    if norms == NH + 2 + 3:
                        root(pool, sty, RMS_EPS, norm_sum_y, 0, pool_y, norm_root_y)
                        pool.tensor_tensor(H2y[:, :, :], H2y[:, :, :], R1[:, :, :], ALU.add).then_inc(hr_done, 1)
                        pool.wait_ge(hr_done, 1)
                yield name

        PACE_X = [(0, 3.0), (2, 0.621), (2, 1.158), (8, 0.8), (19, 0.831), (2, 0.8), (9, 1.352), (6, 0.739),
                  (27, 0.4), (6, 0.4), (29, 1.0), (2, 1.0), (14, 0.739), (8, 0.809), (8, 0.501), (12, 0.242),
                  (0, 2.688)]
        PACE_Y = [(1, 0.45), (15, 0.713), (17, 0.526), (15, 0.81), (4, 0.81), (16, 0.81), (3, 1.146), (12, 0.7),
                  (24, 0.84), (37, 0.75), (2, 0.75), (2, 1.2), (8, 0.587), (8, 1.2), (8, 0.88), (16, 0.88),
                  (3, 0.88), (11, 1.3), (12, 1.3), (14, 1.3), (2, 0.838), (0, 3.0)]

        def order(pace_x, pace_y):
            at = []
            for pace in (pace_x, pace_y):
                whole, t, ends = sum(max(n, 1) * w for n, w in pace), 0.0, []
                for n, w in pace:
                    if n == 0:
                        t += w
                    for _ in range(n):
                        ends.append(t / whole)
                        t += w
                at.append(ends)
            steps = [(t, "x") for t in at[0]] + [(t, "y") for t in at[1]]
            return [side for _, side in sorted(steps, key=lambda step: step[0])]

        X_NAMES = (["split"] * 2 + ["turn"] * 2 + ["project"] * 8 + ["mix"] * (2 * NTI + MIX) + ["rows"] * 2
                   + ["norm"] * 9 + ["turn"] * 3 + ["project"] * 3 + ["maxima"] * (3 * NT) + ["norm", "turn"] * 3
                   + ["attend"] * (3 * NT + 2) + ["rows"] * 2 + ["norm"] * 14 + ["turn"] * 3 + ["project"] * 5
                   + ["slots"] * 8 + ["turn"] * 12)
        Y_NAMES = ["copy"] + (["maxima"] * PER_HEAD + ["norm"]) * 2 + (["maxima"] * PER_HEAD + ["norm"] + ["turn"] * 3) * 2
        Y_NAMES += (["causal"] * (len(CAUSAL) + 2) + ["back"] + ["norm"] * 2 + ["turn"] * 3 + ["project"] * 5
                   + ["norm"] * 8 + ["turn"] * 3 + ["project"] * 5 + ["route"] * 16 + ["turn"] * 3)
        for u in range(NC3 * NG + DOWN):
            Y_NAMES += ["expert"] + ["back"] * (u > NG + DOWN and (u - DOWN) % NG == 1)
        Y_NAMES += ["back"] * 2
        assert len(X_NAMES) == sum(n for n, _ in PACE_X) and len(Y_NAMES) == sum(n for n, _ in PACE_Y), (len(X_NAMES), len(Y_NAMES))
        TURNS = order(PACE_X, PACE_Y)

        def beside_each_other(x, y):
            nx = ny = 0
            for turn in TURNS:
                if turn == "x":
                    if x is not None:
                        assert next(x) == X_NAMES[nx], nx
                    nx += 1
                else:
                    if y is not None:
                        assert next(y) == Y_NAMES[ny], ny
                    ny += 1
            for g in (x, y):
                assert g is None or next(g, None) is None

        def one_round(load, store, x_side, y_side):
            side = lambda g, on: g if on else None
            with nc.Block() as block:
                @block.sync
                def _(sp):
                    if x_side:
                        sp.dma_start(xin, load[0]).then_inc(x_in, 16)
                        sp.dma_start(H[0:LAST, NTI, :], load[1]).then_inc(x_in, 16)
                    if y_side:
                        sp.wait_ge(e_rows, NC3)
                        sp.dma_start(store[0], R1[:, 0:NTI, :]).then_inc(stored, 16)
                        sp.dma_start(store[1], R1[0:LAST, NTI, :]).then_inc(stored, 16)
                        sp.wait_ge(stored, 32)

                @block.gpsimd
                def _(pool):
                    beside_each_other(side(mix_pool(pool, X_NAMES), x_side), side(out_pool(pool, Y_NAMES), y_side))

                @block.tensor
                def _(pe):
                    beside_each_other(side(mix_tensor(pe, y_side), x_side), side(out_tensor(pe), y_side))

                @block.scalar
                def _(act):
                    beside_each_other(side(mix_scalar(act, y_side), x_side), side(out_scalar(act), y_side))

                @block.vector
                def _(dve):
                    beside_each_other(side(mix_vector(dve, y_side), x_side), side(out_vector(dve), y_side))

            nc.all_engine_barrier(sems_to_clear=range(min(loop_sems), max(loop_sems) + 1))

        def loads(b):
            return (x[bass.ds(b, 1), :, :, :].rearrange("a o (t p) f -> p (a o t) f", p=P),
                    txt[bass.ds(b, 1), :, :].rearrange("a t f -> (a t) f"))

        def stores(b):
            return (out[bass.ds(b, 1), 0:T_IMG, :].rearrange("a (t p) f -> p (a t) f", p=P),
                    out[bass.ds(b, 1), T_IMG:T, :].rearrange("a t f -> (a t) f"))

        one_round(loads(0), None, True, False)
        with nc.Fori(1, B) as b:
            one_round(loads(b), stores(b - 1), True, True)
        one_round(None, stores(B - 1), False, True)


_INS = ['x', 'txt', 'L0_tok_d_gamma_batched', 'L0_tok_Wq', 'L0_tok_bq', 'L0_tok_Wk', 'L0_tok_bk', 'L0_tok_Wv',
        'L0_tok_bv', 'L0_tok_Wo', 'L0_tok_bo', 'L0_tok_prelu_a', 'L0_attn_Wq', 'L0_attn_Wk', 'L0_ffn_ln1_w',
        'L0_ffn_ln2_w', 'L0_ffn_wq', 'L0_ffn_wk', 'L0_ffn_wv', 'L0_ffn_wo', 'L0_ffn_router_w', 'L0_ffn_w1',
        'L0_ffn_w2', 'L0_ffn_w3']


def _constants():
    import numpy as np

    i = np.arange(P)
    above = np.where(i[None, :] > i[:, None], np.float32(-1e30), np.float32(0))
    inv_freq = 1.0 / 10000.0 ** (np.arange(0, HD, 2, dtype=np.float32) / HD)
    freqs = np.outer(np.arange(TP, dtype=np.float32), inv_freq.astype(np.float32))
    emb = np.concatenate([freqs, freqs], axis=-1)
    table = lambda a: np.ascontiguousarray(a.astype(np.float32).reshape(NT, P, HD).transpose(1, 0, 2))
    owner = np.arange(NG * P) // HID
    sel = (owner[None, :] == (np.arange(16) % NE)[:, None]).astype(np.float32)
    e = np.arange(NE)
    tri = np.tile((e[None, :] < e[:, None]).astype(np.float32).reshape(1, -1), (P, 1))
    return {
        "c_ident": np.eye(P, dtype=np.float32),
        "c_mask": np.ascontiguousarray(np.stack([above, above.T], axis=1)),
        "c_cos": table(np.cos(emb)),
        "c_sin": table(np.sin(emb)),
        "c_sel": sel,
        "c_tri": tri,
    }


def kernel(**inputs):
    import numpy as np
    import concourse.bacc as bacc
    from concourse.bass_utils import run_bass_kernel_spmd

    nc = bacc.Bacc("TRN2", target_bir_lowering=False, num_devices=1)
    arrays, args = {}, []
    given = {n: np.asarray(inputs[n]) for n in _INS}
    given['L0_tok_prelu_a'] = given['L0_tok_prelu_a'].reshape(1, 1)
    given.update(_constants())
    for name, a in given.items():
        a = np.ascontiguousarray(a)
        arrays[f"in_{name}"] = a
        args.append(nc.dram_tensor(f"in_{name}", a.shape, mybir.dt.from_np(a.dtype), kind="ExternalInput").ap())
    args.append(nc.dram_tensor("out_0", (B, T, C), F32, kind="ExternalOutput").ap())
    early_fusion_kernel(nc, *args)
    res = run_bass_kernel_spmd(nc, [arrays], core_ids=[0])
    return res.results[0]["out_0"]
```
